# Optimizing a Trainium2 kernel written in Bass

```python
import numpy as np
import jax
import jax.numpy as jnp

def _softmax(x, axis=-1):
    return jax.nn.softmax(x, axis=axis)

def _gelu(x):
    return jax.nn.gelu(x, approximate=True)

def _silu(x):
    return jax.nn.silu(x)

def _sigmoid(x):
    return jax.nn.sigmoid(x)

def _layernorm(x, axis=-1, eps=1e-05):
    m = jnp.mean(x, axis=axis, keepdims=True)
    v = jnp.var(x, axis=axis, keepdims=True)
    return (x - m) / jnp.sqrt(v + eps)

def _scatter_add(tgt, idx, src, axis=0):
    return tgt.at[idx].add(src)

def _segment_sum(src, seg, n):
    return jax.ops.segment_sum(src, seg, n)
kernel_name = 'mk_seq_preln_d1_jaxref_r4_3eaa76'

def setup_inputs(seed: int=0):
    np.random.seed(seed)
    _w = jnp.asarray

    def _L0_attn_setup():
        import jax, jax.numpy as jnp
        import numpy as np
        D = 256
        H = 8
        NUM_LEVELS = 3
        CHUNK0 = 128
        OVERLAP = 64

        def _mha(x, Win, bin_, Wout, bout):
            B, T, _ = x.shape
            dh = D // H
            qkv = x @ Win.T + bin_
            q, k, v = jnp.split(qkv, 3, axis=-1)
            q = q.reshape(B, T, H, dh)
            k = k.reshape(B, T, H, dh)
            v = v.reshape(B, T, H, dh)
            scale = 1.0 / jnp.sqrt(jnp.asarray(dh, x.dtype))
            scores = jnp.einsum('bqhd,bkhd->bhqk', q, k) * scale
            attn = jax.nn.softmax(scores, axis=-1)
            out = jnp.einsum('bhqk,bkhd->bqhd', attn, v).reshape(B, T, D)
            return out @ Wout.T + bout

        def _forward(x, params):
            B, L, _ = x.shape
            chunk = min(CHUNK0, L)
            cur = x
            for level in range(NUM_LEVELS):
                stride = chunk - OVERLAP
                outs = [_mha(cur[:, i:min(i + chunk, L)], *params[level]) for i in range(0, L, stride)]
                cur = jnp.concatenate(outs, axis=1)[:, :L]
                chunk *= 2
            return cur
        key = jax.random.key(seed)
        ks = jax.random.split(key, 1 + 4 * NUM_LEVELS)
        inp = {'x': jax.random.normal(ks[0], (4, 2048, D), dtype=jnp.float32)}
        for l in range(NUM_LEVELS):
            k0, k1, k2, k3 = ks[1 + 4 * l:5 + 4 * l]
            inp[f'Win{l}'] = jax.random.normal(k0, (3 * D, D), dtype=jnp.float32) * 0.02
            inp[f'bin{l}'] = jax.random.normal(k1, (3 * D,), dtype=jnp.float32) * 0.02
            inp[f'Wout{l}'] = jax.random.normal(k2, (D, D), dtype=jnp.float32) * 0.02
            inp[f'bout{l}'] = jax.random.normal(k3, (D,), dtype=jnp.float32) * 0.02
        return inp
    _L0_attn_in = _L0_attn_setup()

    def _L0_ffn_setup():
        import jax, jax.numpy as jnp
        import numpy as np
        E = 8
        K = 2
        key = jax.random.key(seed)
        ks = jax.random.split(key, 8)
        B, T, d = (4, 512, 256)
        h = 4 * d // E
        s = 0.02
        X = jax.random.normal(ks[0], (B, T, d), jnp.float32)
        routing_W = jax.random.normal(ks[1], (E, d), jnp.float32) * s
        expert_bias = jnp.zeros((E,), jnp.float32)
        sW1 = jax.random.normal(ks[2], (d, h), jnp.float32) * s
        sb1 = jnp.zeros((h,), jnp.float32)
        sW2 = jax.random.normal(ks[3], (h, d), jnp.float32) * s
        sb2 = jnp.zeros((d,), jnp.float32)
        rW1 = jax.random.normal(ks[4], (E, d, h), jnp.float32) * s
        rb1 = jnp.zeros((E, h), jnp.float32)
        rW2 = jax.random.normal(ks[5], (E, h, d), jnp.float32) * s
        rb2 = jnp.zeros((E, d), jnp.float32)
        return dict(X=X, routing_W=routing_W, expert_bias=expert_bias, sW1=sW1, sb1=sb1, sW2=sW2, sb2=sb2, rW1=rW1, rb1=rb1, rW2=rW2, rb2=rb2)
    _L0_ffn_in = _L0_ffn_setup()
    _d = {'L0_attn_x': _L0_attn_in['x'], 'L0_attn_Win0': _L0_attn_in['Win0'], 'L0_attn_bin0': _L0_attn_in['bin0'], 'L0_attn_Wout0': _L0_attn_in['Wout0'], 'L0_attn_bout0': _L0_attn_in['bout0'], 'L0_attn_Win1': _L0_attn_in['Win1'], 'L0_attn_bin1': _L0_attn_in['bin1'], 'L0_attn_Wout1': _L0_attn_in['Wout1'], 'L0_attn_bout1': _L0_attn_in['bout1'], 'L0_attn_Win2': _L0_attn_in['Win2'], 'L0_attn_bin2': _L0_attn_in['bin2'], 'L0_attn_Wout2': _L0_attn_in['Wout2'], 'L0_attn_bout2': _L0_attn_in['bout2'], 'L0_ffn_routing_W': _L0_ffn_in['routing_W'], 'L0_ffn_expert_bias': _L0_ffn_in['expert_bias'], 'L0_ffn_sW1': _L0_ffn_in['sW1'], 'L0_ffn_sb1': _L0_ffn_in['sb1'], 'L0_ffn_sW2': _L0_ffn_in['sW2'], 'L0_ffn_sb2': _L0_ffn_in['sb2'], 'L0_ffn_rW1': _L0_ffn_in['rW1'], 'L0_ffn_rb1': _L0_ffn_in['rb1'], 'L0_ffn_rW2': _L0_ffn_in['rW2'], 'L0_ffn_rb2': _L0_ffn_in['rb2']}
    _x0 = _d['L0_attn_x']
    _d['L0_attn_x'] = jax.random.normal(jax.random.fold_in(jax.random.key(seed), 1), (8, 1024, 256), dtype=_x0.dtype)
    del _x0
    return _d

def reference(L0_attn_x, L0_attn_Win0, L0_attn_bin0, L0_attn_Wout0, L0_attn_bout0, L0_attn_Win1, L0_attn_bin1, L0_attn_Wout1, L0_attn_bout1, L0_attn_Win2, L0_attn_bin2, L0_attn_Wout2, L0_attn_bout2, L0_ffn_routing_W, L0_ffn_expert_bias, L0_ffn_sW1, L0_ffn_sb1, L0_ffn_sW2, L0_ffn_sb2, L0_ffn_rW1, L0_ffn_rb1, L0_ffn_rW2, L0_ffn_rb2):

    def _L0_attn_ref(x, Win0, bin0, Wout0, bout0, Win1, bin1, Wout1, bout1, Win2, bin2, Wout2, bout2):
        import jax, jax.numpy as jnp
        import numpy as np
        D = 256
        H = 8
        NUM_LEVELS = 3
        CHUNK0 = 128
        OVERLAP = 64

        def _mha(x, Win, bin_, Wout, bout):
            B, T, _ = x.shape
            dh = D // H
            qkv = x @ Win.T + bin_
            q, k, v = jnp.split(qkv, 3, axis=-1)
            q = q.reshape(B, T, H, dh)
            k = k.reshape(B, T, H, dh)
            v = v.reshape(B, T, H, dh)
            scale = 1.0 / jnp.sqrt(jnp.asarray(dh, x.dtype))
            scores = jnp.einsum('bqhd,bkhd->bhqk', q, k) * scale
            attn = jax.nn.softmax(scores, axis=-1)
            out = jnp.einsum('bhqk,bkhd->bqhd', attn, v).reshape(B, T, D)
            return out @ Wout.T + bout

        def _forward(x, params):
            B, L, _ = x.shape
            chunk = min(CHUNK0, L)
            cur = x
            for level in range(NUM_LEVELS):
                stride = chunk - OVERLAP
                outs = [_mha(cur[:, i:min(i + chunk, L)], *params[level]) for i in range(0, L, stride)]
                cur = jnp.concatenate(outs, axis=1)[:, :L]
                chunk *= 2
            return cur
        params = [(Win0, bin0, Wout0, bout0), (Win1, bin1, Wout1, bout1), (Win2, bin2, Wout2, bout2)]
        return _forward(x, params)

    def _L0_ffn_ref(X, routing_W, expert_bias, sW1, sb1, sW2, sb2, rW1, rb1, rW2, rb2):
        import jax, jax.numpy as jnp
        import numpy as np
        E = 8
        K = 2
        B, T, d = X.shape
        shared = jax.nn.silu(X @ sW1 + sb1) @ sW2 + sb2
        logits = jnp.einsum('btd,ed->bte', X, routing_W) + expert_bias
        activation = jnp.sqrt(jax.nn.softplus(logits))
        top_vals, top_idx = jax.lax.top_k(activation, K)
        combine = jnp.sum(jax.nn.one_hot(top_idx, E, dtype=X.dtype) * top_vals[..., None], axis=-2)
        Xf = X.reshape(-1, d)
        cf = combine.reshape(-1, E)
        hdn = jax.nn.silu(jnp.einsum('nd,edh->enh', Xf, rW1) + rb1[:, None, :])
        y = jnp.einsum('enh,ehd->end', hdn, rW2) + rb2[:, None, :]
        routed = jnp.einsum('ne,end->nd', cf, y).reshape(B, T, d)
        return shared + routed
    x = L0_attn_x
    x = x + _L0_attn_ref(_layernorm(x, axis=-1), L0_attn_Win0, L0_attn_bin0, L0_attn_Wout0, L0_attn_bout0, L0_attn_Win1, L0_attn_bin1, L0_attn_Wout1, L0_attn_bout1, L0_attn_Win2, L0_attn_bin2, L0_attn_Wout2, L0_attn_bout2)
    x = x + _L0_ffn_ref(_layernorm(x, axis=-1), L0_ffn_routing_W, L0_ffn_expert_bias, L0_ffn_sW1, L0_ffn_sb1, L0_ffn_sW2, L0_ffn_sb2, L0_ffn_rW1, L0_ffn_rb1, L0_ffn_rW2, L0_ffn_rb2)
    return x

_drawn_inputs = setup_inputs


def setup_inputs(seed=0):
    import zlib

    import numpy as np

    out = dict(_drawn_inputs(seed))
    spreads = {'L0_ffn_expert_bias': (0.0, 0.8),
     'L0_ffn_sb1': (0.0, 2.0),
     'L0_ffn_sb2': (0.0, 2.0),
     'L0_ffn_rb1': (0.0, 2.0),
     'L0_ffn_rb2': (0.0, 2.0)}
    factors = {'L0_attn_Win0': 8.0,
     'L0_attn_bin0': 8.0,
     'L0_attn_Wout0': 8.0,
     'L0_attn_bout0': 8.0,
     'L0_attn_Win1': 8.0,
     'L0_attn_bin1': 8.0,
     'L0_attn_Wout1': 8.0,
     'L0_attn_bout1': 8.0,
     'L0_attn_Win2': 8.0,
     'L0_attn_bin2': 4.592,
     'L0_attn_Wout2': 5.248,
     'L0_attn_bout2': 64.0,
     'L0_ffn_routing_W': 8.0,
     'L0_ffn_sW1': 24.86,
     'L0_ffn_sW2': 8.0,
     'L0_ffn_rW1': 8.0,
     'L0_ffn_rW2': 8.0}
    for name, (base, spread) in spreads.items():
        noise = np.random.default_rng([zlib.crc32(name.encode()), seed]).standard_normal(out[name].shape)
        drawn = base * np.exp(spread * noise) if base else spread * noise
        out[name] = jnp.asarray(drawn.astype(out[name].dtype))
    for name, factor in factors.items():
        out[name] = (out[name] * factor).astype(out[name].dtype)
    return out
```

```python
from contextlib import ExitStack

import concourse.bass as bass
from concourse import mybir
from concourse.alu_op_type import AluOpType as ALU

F32 = mybir.dt.float32
F32R = mybir.dt.float32r
U32 = mybir.dt.uint32
ACT = mybir.ActivationFunctionType
AX_X = mybir.AxisListType.X

P = 128
BANK = 512
LN_EPS = 1e-5
OVERLAP = 64
SENTINEL = -3.0e38
EXP_TANH = "exp_and_others"
W_STEP, W_NORM, W_SMAX, W_DENSE, W_STACK, W_LEVEL = (1, 1, 1.5), 2, (0.3, 1, 1.5), 0.4, 8, 4
LOG1P_TERMS = (13, 11, 9, 7, 5, 3)


class Level:

    def __init__(self, width, out_len):
        self.width = width
        self.stride = width - OVERLAP
        self.windows = -(-out_len // width)
        self.out_len = out_len
        self.tokens = (self.windows - 1) * self.stride + width
        self.ktiles = width // P
        self.heads_per_item = BANK // width
        self.items = 4 // self.heads_per_item
        self.per_unit = BANK // width
        self.units = [list(range(u, min(u + self.per_unit, self.windows)))
                      for u in range(0, self.windows, self.per_unit)]
        self.vtiles = self.windows * self.ktiles

    def queries(self, w):
        return min(self.width, self.out_len - w * self.width)

    def unit_len(self, u):
        return sum(self.queries(w) for w in self.units[u])

    def steps(self, u):
        return [(w, kt) for w in self.units[u] for kt in range(self.ktiles)]

    def key_chunks(self):
        return [(c, min(BANK, self.tokens - c)) for c in range(0, self.tokens, BANK)]


def make_levels(seq, width0, n):
    widths = [width0 << i for i in range(n)]
    out_len, levels = seq, []
    for w in reversed(widths):
        lev = Level(w, out_len)
        levels.append(lev)
        out_len = lev.tokens
    return levels[::-1]


def attention_plan(levels, out_tiles):
    plan = [("T1", kt) for kt in range(2)] + [("HOOK", 1)]
    for l, lev in enumerate(levels):
        for hg in range(2):
            for c in range(len(lev.key_chunks())):
                plan += [("K", l, hg, c), ("HOOK", W_DENSE)]
        for u in range(2):
            for hg in range(2):
                plan += [("Q", l, hg, u), ("HOOK", W_DENSE)]
        for v in range(0, lev.vtiles, 2):
            plan += [("V", l, v), ("HOOK", W_DENSE)]
        plan.append(("HOOK", W_STACK))

        if l == len(levels) - 1:
            plan.append(("L1",))

        def smax(n):
            return [[("S", l, n, j, i) for i in range(lev.items)] for j in range(len(lev.steps(n // 2)))]

        def probs(n):
            return [[("ST", l, n, j, i) for i in range(lev.items)] for j in range(len(lev.steps(n // 2)))]

        for j, items in enumerate(smax(0)):
            plan += items
            plan.append(("HOOK", W_SMAX[l]))
        for j, items in enumerate(smax(1)):
            plan += items
            if j == 0:
                plan.append(("MT", l, 0))
            plan.append(("HOOK", W_SMAX[l]))
        owed = []
        for n in range(4):
            ahead = smax(n + 2) if n < 2 else []
            for j, items in enumerate(probs(n)):
                if j < len(ahead):
                    for a, s in zip(items, ahead[j]):
                        plan += [a, s]
                else:
                    plan += items
                plan += owed
                owed = [("PV", l, n, j)]
                if j == len(lev.steps(n // 2)) - 1:
                    owed.append(("NORM", l, n))
                if j == 0 and n < 3:
                    plan.append(("MT", l, n + 1))
                plan.append(("HOOK", W_NORM if n and j == 0 else W_STEP[l]))
                if l == len(levels) - 1 and n == 1:
                    plan += {0: [("L1a",)], 2: [("L1b",)]}.get(j, [])
        plan += owed
        plan.append(("HOOK", W_LEVEL))
    for t in range(0, out_tiles, 2):
        plan.append(("OP", t))
    return plan


def expert_plan(groups, pairs):
    plan = [("F1", 0), ("FN", 0), ("T2", 0), ("LG", 0), ("LT", 0), ("TP", 0), ("CW", 0), ("GAP", 0), ("CT", 0)]
    for g in range(groups):
        more = g + 1 < groups
        for p in range(pairs):
            plan.append(("W1", g, p))
            if more and p in (1, 3):
                plan.append(("F1" if p == 1 else "FN", g + 1))
        plan += [("T2", g + 1), ("LG", g + 1)] if more else []
        plan.append(("W2", g, 0))
        plan += [("LT", g + 1), ("TP", g + 1), ("CW", g + 1), ("GAP", g + 1)] if more else []
        plan.append(("W2", g, 1))
        plan += [("CT", g + 1)] if more else []
    return plan


COST = dict(F1=0, FN=0, T2=0.5, LG=0.7, LT=0.2, TP=0, CW=0, GAP=0, CT=0.3, W1=1.6, W2=4)
LATENCY = {("F1", "FN"): 2, ("FN", "T2"): 1.5, ("T2", "LG"): 2, ("LG", "LT"): 1.5, ("LT", "TP"): 1,
           ("CW", "GAP"): 4, ("GAP", "CT"): 4, ("GAP", "W2"): 0, ("CT", "W1"): 2, ("W1", "W1"): 1,
           ("W1", "W2"): 2.5, ("TP", "CW"): 0.5}


def place_tasks(tasks, hooks):
    scale = sum(COST[t[0]] for t in tasks) / sum(hooks)

    def price(room, some):
        load = sum(COST[t[0]] for t in some)
        stall = sum(LATENCY.get((a[0], c[0]), 0) for a, c in zip(some, some[1:]))
        return (load - room * scale) ** 2 + 2.0 * stall

    best = {0: (0.0, None)}
    trail = []
    for room in hooks:
        new = {}
        for i, (v, _) in best.items():
            for j in range(i, min(i + 6, len(tasks)) + 1):
                w = v + price(room, tasks[i:j])
                if j not in new or w < new[j][0]:
                    new[j] = (w, i)
        trail.append(new)
        best = new
    j, out_ = len(tasks), []
    for new in reversed(trail):
        i = new[j][1]
        out_.append([t for t in tasks[i:j] if t[0] != "GAP"])
        j = i
    return out_[::-1]


def block_kernel(nc, x, winT, wout0, wout1, woutT, bins, bouts, wrT, ebias,
                 sw1, sb1, sw2, sb2, rw1, rb1T, rw2, rb2, out):
    B, L, D = x.shape
    H, E = rb1T.shape
    HEADS, DH = 8, 32
    SCALE = float(DH) ** -0.5
    KD = D // P
    TT = L // P
    E1 = E + 1
    C3 = 3 * E1
    GT = 2
    G = TT // GT
    GN = GT * P
    PAIRS = (E1 + 1) // 2
    levels = make_levels(L, 128, 3)
    assert KD == 2 and HEADS == 8 and H == P and all(len(v.units) == 2 for v in levels)
    LT0 = levels[0].tokens // P

    attn = attention_plan(levels, TT)
    tasks = expert_plan(G, PAIRS)
    experts = [task for task in tasks if task[0] != "GAP"]
    at_hook = place_tasks(tasks, [op[1] for op in attn if op[0] == "HOOK"])

    A_KINDS = ("T1", "K", "Q", "V", "S", "MT", "OP")
    a_items = [op for op in attn if op[0] in A_KINDS]
    a_index = {op: i for i, op in enumerate(a_items)}
    NA = len(a_items)
    a_by_act = [op for op in a_items if op[0] == "V"]
    a_by_dve = [op for op in a_items if op[0] != "V"]
    a_act_no = {op: i + 1 for i, op in enumerate(a_by_act)}
    a_dve_no = {op: i + 1 for i, op in enumerate(a_by_dve)}
    hi_ops = [op for op in a_items if op[0] in ("T1", "K", "Q")]
    hi_no = {op: i + 1 for i, op in enumerate(hi_ops)}
    st_items = [op for op in attn if op[0] == "ST"]
    st_no = {op: i + 1 for i, op in enumerate(st_items)}
    NST = len(st_items)
    pv_ops = [op for op in attn if op[0] == "PV"]
    pv_no = {op: i + 1 for i, op in enumerate(pv_ops)}
    NPV = len(pv_ops)
    norm_no = {op: i + 1 for i, op in enumerate([op for op in attn if op[0] == "NORM"])}
    NN = len(norm_no)
    mt_no = {op: i + 1 for i, op in enumerate([op for op in attn if op[0] == "MT"])}
    NM = len(mt_no)
    f_items = []
    for op in experts:
        if op[0] in ("T2", "LG", "LT", "CT", "W2"):
            f_items.append(op)
        if op[0] == "W1":
            f_items += [("CB",) + op[1:], op]
    f_index = {op: i for i, op in enumerate(f_items)}
    NF = len(f_items)
    f_act_no = {op: i + 1 for i, op in enumerate([op for op in f_items if op[0] in ("LG", "CB")])}
    f_dve_no = {op: i + 1 for i, op in enumerate([op for op in f_items if op[0] not in ("LG", "CB")])}
    NFA, NFD = len(f_act_no), len(f_dve_no)
    assert NA % 2 == 0 and NST % 2 == 0 and NPV % 2 == 0 and NF % 2 == 0
    STACK = 12 * 16
    NL = len(levels)
    MAXPOS = max(v.windows * v.width for v in levels)
    MAXTOK = max(v.tokens for v in levels)

    with ExitStack() as ctx:
        def sb(name, shape, dt=F32):
            return ctx.enter_context(nc.sbuf_tensor(name, shape, dt))

        def sem(name):
            return ctx.enter_context(nc.semaphore(name))

        wl_hi = sb("wl_hi", [P, NL, KD, 3 * D], F32R)
        wl_lo = sb("wl_lo", [P, NL, KD, 3 * D], F32R)
        wo_hi = sb("wo_hi", [P, KD, D], F32R)
        wo_lo = sb("wo_lo", [P, KD, D], F32R)
        w1_hi = sb("w1_hi", [P, KD, E1 * H], F32R)
        w1_lo = sb("w1_lo", [P, KD, E1 * H], F32R)
        w2_sb = sb("w2_sb", [P, E1, D])
        wr_hi = sb("wr_hi", [P, KD, E], F32R)
        wr_lo = sb("wr_lo", [P, KD, E], F32R)
        b2_st = sb("b2_st", [C3, D], F32R)
        sel = sb("sel", [C3, E1], F32R)
        b1c = sb("b1c", [P, E1])
        b1h = sb("b1h", [P, E1])
        ebc = sb("ebc", [E, 1])
        bcol = sb("bcol", [P, NL, 6])
        t0c = sb("t0c", [P, NL, KD])
        ident = sb("ident", [P, P])
        ones = sb("ones", [P, DH])
        brow = sb("brow", [P, D])
        xt_hi = sb("xt_hi", [P, KD, MAXPOS], F32R)
        xt_lo = sb("xt_lo", [P, KD, MAXPOS], F32R)
        kpack = sb("kpack", [P, 2, 2, MAXPOS])
        qpack = sb("qpack", [P, 2, 2, 2, BANK])
        kst = sb("kst", [98, HEADS, MAXTOK], F32R)
        qst = sb("qst", [98, 2, HEADS, BANK], F32R)
        v_sb = sb("v_sb", [P, 8, D])
        xln = sb("xln", [P, LT0, D])
        x1 = sb("x1", [P, TT, D])
        mx = sb("mx", [P, 2, 16])
        rows = sb("rows", [P, 2 * P])
        st1 = sb("st1", [P, LT0, 6])
        mv1 = sb("mv1", [P, LT0, 2])
        rs1 = sb("rs1", [P, LT0])
        st2 = sb("st2", [P, GT, 6])
        mv2 = sb("mv2", [P, GT, 2])
        rs2 = sb("rs2", [P, GT])
        mhalf = sb("mhalf", [P, 4])
        half = sb("half", [P, GT, E])
        mone = sb("mone", [P, 1])
        rcol = sb("rcol", [P, BANK // DH])
        xn2 = sb("xn2", [P, GT, D])
        x2_hi = sb("x2_hi", [P, KD, GN], F32R)
        x2_lo = sb("x2_lo", [P, KD, GN], F32R)
        lgt = rows[0:E, 0:GN]
        nm_hi = rows[32:48, 0:P]
        nm_lo = rows[32:48, P:2 * P]
        lgp = sb("lgp", [P, GT, 16])
        rep = sb("rep", [P, GT, 16])
        m8a = sb("m8a", [P, GT, 8])
        m8 = sb("m8", [P, GT, 8])
        mask = sb("mask", [P, GT, E])
        sp = sb("sp", [P, 6, GT, E])
        cw = sb("cw", [P, 2, GT, E])
        cst = sb("cst", [P, GT, C3], F32R)
        ct = sb("ct", [C3, GN], F32R)
        th = sb("th", [P, 2, 2, GN])
        hs = sb("hs", [P, E1, GN])
        probs = qpack[:, :, :, :, :].rearrange("p a u b c -> p (a u b c)").rearrange("p (s n) -> p s n", s=2)
        kflat = kpack[:, :, :, :].rearrange("p a b c -> p (a b c)")
        xres = kflat[:, 0:TT * D].rearrange("p (t d) -> p t d", t=TT)
        rinv = kflat[:, TT * D:TT * D + BANK]
        o_n = kflat[:, TT * D + BANK:TT * D + 2 * BANK]
        ones_b = ones[:, :]

        def bank(name):
            return ctx.enter_context(nc.psum_tensor(name, [P, BANK], F32))

        a_bank = [bank("a0"), bank("a1")]
        st_bank = [bank("st0"), bank("st1b")]
        f_bank = [bank("f0"), bank("f1")]
        o_bank, sum_bank = bank("o"), bank("sum")

        s_w = sem("s_w")
        s_prep_pe, s_prep_act, s_prep_dve = sem("s_prep_pe"), sem("s_prep_act"), sem("s_prep_dve")
        s_prep_pool = sem("s_prep_pool")
        s_b2 = sem("s_b2")
        a_ready = sem("a_ready")
        a_act = sem("a_act")
        a_dve = sem("a_dve")
        hi_done = sem("hi_done")
        st_ready = sem("st_ready")
        exp_done = sem("exp_done")
        pv_done = sem("pv_done")
        rinv_c = sem("rinv_c")
        on_done = sem("on_done")
        on_hi = sem("on_hi")
        on_lo = sem("on_lo")
        nmh_done = sem("nmh_done")
        stack_k, stack_q = sem("stack_k"), sem("stack_q")
        rows_in = sem("rows_in")
        xln_in, xres_in = sem("xln_in"), sem("xres_in")
        xb_done = sem("xb_done")
        bn1, ag1, rs1_add, rs1_pow, xn1 = sem("bn1"), sem("ag1"), sem("rs1_add"), sem("rs1_pow"), sem("xn1")
        f_ready, f_act, f_dve = sem("f_ready"), sem("f_act"), sem("f_dve")
        bn2, ag2, rs2_add, rs2_pow, xn2_done = sem("bn2"), sem("ag2"), sem("rs2_add"), sem("rs2_pow"), sem("xn2_done")
        x2hi_done = sem("x2hi_done")
        top_c = sem("top_c")
        mask_done = sem("mask_done")
        abs_done, e_done = sem("abs_done"), sem("e_done")
        sp_c = sem("sp_c")
        cw_c = sem("cw_c")
        th_done = sem("th_done")
        t1_done = sem("t1_done")
        out_done = sem("out_done")
        passed = sem("passed")

        N_SP = len(LOG1P_TERMS) + 7
        N_TOP = 2 + 1 + 2

        def wait(eng, s, b, per_batch, n, apart=False):
            v = b * per_batch + n
            if not isinstance(v, int) or v > 0:
                eng.wait_ge(s, v)
            if apart and not isinstance(v, int):
                eng.sem_inc(passed, 1)

        def streams(engine_loop, body):
            body(0, None)
            body(1, 0)
            with engine_loop(2, B - 1) as i:
                body(i, i - 1)
            body(B - 1, B - 2)
            body(None, B - 1)

        def walk(attn_op, expert_op, ba, bf):
            k = 0
            if isinstance(ba, int) and ba == 0:
                attn_op(("L1",), 0)
                attn_op(("L1a",), 0)
                attn_op(("L1b",), 0)
            if ba is None:
                for op in experts:
                    expert_op(op, bf)
                return
            for op in attn:
                if op[0] == "HOOK":
                    if bf is not None:
                        for f in at_hook[k]:
                            expert_op(f, bf)
                    k += 1
                elif op[0] in ("L1", "L1a", "L1b"):
                    if not (isinstance(ba, int) and ba == B - 1):
                        attn_op(op, ba + 1)
                else:
                    attn_op(op, ba)

        def spread(col, n):
            return bass.AP(tensor=col.tensor, offset=col.offset, ap=[col.ap[0], [0, n]])

        def heads_of(l, i):
            n = levels[l].heads_per_item
            return range(i * n, (i + 1) * n)

        stage0 = kpack[:, :, :, :].rearrange("p a b c -> p (a b c)")
        stage1 = qpack[:, :, :, :, :].rearrange("p a u b c -> p (a u b c)")
        win_st = [stage0[:, i * 2 * 768:(i + 1) * 2 * 768].rearrange("p (k n) -> p k n", k=2) for i in range(2)]
        wout_st = [stage0[:, 3072:3584].rearrange("p (k n) -> p k n", k=2),
                   stage0[:, 3584:4096].rearrange("p (k n) -> p k n", k=2)]
        win2_st = stage1[:, 0:1536].rearrange("p (k n) -> p k n", k=2)
        woutT_st = [stage1[:, 1536 + i * 512:2048 + i * 512].rearrange("p (k n) -> p k n", k=2) for i in range(3)]
        bins_st = stage1[:, 3072:3072 + 18].rearrange("p (l m) -> p l m", l=3)
        bouts_st = stage1[:, 3096:3096 + 6].rearrange("p (l m) -> p l m", l=3)
        wr_st = stage1[:, 3104:3120].rearrange("p (k n) -> p k n", k=2)
        bo2_st = stage1[:, 3120:3120 + 256]
        colb = stage1[:, 3376:3376 + 256].rearrange("p (k n) -> p k n", k=2)
        w1_st = hs[:, :, :].rearrange("p e n -> p (e n)").rearrange("p (k n) -> p k n", k=2)
        b2_stg = x1[0:C3, 0, :]
        b2_hi = x1[0:C3, 1, :]
        b2_lo = x1[0:C3, 2, :]
        N_W = 0

        block = ctx.enter_context(nc.Block())

        loads = [
            (win_st[0], winT[0].rearrange("(k p) n -> p k n", p=P)),
            (win_st[1], winT[1].rearrange("(k p) n -> p k n", p=P)),
            (win2_st, winT[2].rearrange("(k p) n -> p k n", p=P)),
            (wout_st[0], wout0.rearrange("(k p) n -> p k n", p=P)),
            (wout_st[1], wout1.rearrange("(k p) n -> p k n", p=P)),
            (woutT_st[0], woutT[0].rearrange("(k p) n -> p k n", p=P)),
            (woutT_st[1], woutT[1].rearrange("(k p) n -> p k n", p=P)),
            (woutT_st[2], woutT[2].rearrange("(k p) n -> p k n", p=P)),
            (bins_st[:, 0, :], bins[0]),
            (bins_st[:, 1, :], bins[1]),
            (bins_st[:, 2, :], bins[2]),
            (bouts_st[:, 0, :], bouts[0]),
            (bouts_st[:, 1, :], bouts[1]),
            (bo2_st, bass.AP(tensor=bouts[2].tensor, offset=bouts[2].offset, ap=[[0, P], [1, D]])),
            (wr_st, wrT.rearrange("(k p) n -> p k n", p=P)),
            (ebc[:, :], ebias.rearrange("(e a) -> e a", a=1)),
            (b1c[:, 0:E], rb1T),
            (b1c[:, E:E1], sb1.rearrange("(h a) -> h a", a=1)),
            (w2_sb[:, 0:E, :], rw2.rearrange("e h d -> h e d")),
            (w2_sb[:, E, :], sw2),
        ] + [
            (w1_st[:, k, 0:E * H].rearrange("p (e h) -> p e h", e=E),
             rw1.rearrange("e (k p) h -> k p e h", p=P)[k]) for k in range(KD)
        ] + [
            (w1_st[:, :, E * H:], sw1.rearrange("(k p) h -> p k h", p=P)),
        ] + [
            (b2_stg[r * E1:r * E1 + E, :], rb2) for r in range(3)
        ] + [
            (b2_stg[r * E1 + E:(r + 1) * E1, :], sb2.rearrange("(a n) -> a n", a=1)) for r in range(3)
        ]
        ALL_LOADS = 16 * len(loads)

        @block.sync
        def _(sp_):
            for dst, src in loads:
                sp_.dma_start(dst, src).then_inc(s_w, 16)
            sp_.wait_ge(s_b2, 2)
            sp_.dma_start(b2_st[0:2 * E1, :].bitcast(F32), b2_hi[0:2 * E1, :]).then_inc(s_b2, 16)
            sp_.dma_start(b2_st[2 * E1:C3, :].bitcast(F32), b2_lo[2 * E1:C3, :]).then_inc(s_b2, 16)

            def attn_op(op, b):
                kind = op[0]
                if kind == "L1":
                    wait(sp_, a_ready, b, NA, 2 - NA)
                    sp_.dma_start(xln[:, :, :], x[b][0:LT0 * P].rearrange("(t p) d -> p t d", p=P))\
                        .then_inc(xln_in, 16)
                if op == ("S", NL - 1, 1, 0, 0):
                    wait(sp_, stack_k, b, NL * STACK, NL * STACK)
                    sp_.dma_start(xres[:, :, :], x[b].rearrange("(t p) d -> p t d", p=P)).then_inc(xres_in, 16)
                if kind == "K" and op == [o for o in a_items if o[0] == "K" and o[1] == op[1]][-1]:
                    wait(sp_, a_dve, b, len(a_by_dve), a_dve_no[op])
                    n = levels[op[1]].tokens
                    for r, part in enumerate((0, 0, 1)):
                        for g in range(4):
                            sp_.dma_start(kst[32 * r:32 * r + 32, g:8:4, 0:n].bitcast(F32),
                                          kpack[32 * g:32 * g + 32, part, :, 0:n]).then_inc(stack_k, 16)
                if kind == "Q" and op == [o for o in a_items if o[0] == "Q" and o[1] == op[1]][-1]:
                    wait(sp_, a_dve, b, len(a_by_dve), a_dve_no[op])
                    for r, part in enumerate((0, 1, 0)):
                        for g in range(4):
                            sp_.dma_start(
                                qst[32 * r:32 * r + 32, :, :, :].bitcast(F32)
                                .rearrange("p u h q -> p (u h) q")[:, g:16:4, :],
                                qpack[32 * g:32 * g + 32, part, :, :, :].rearrange("p u b q -> p (u b) q")).then_inc(stack_q, 16)
                if kind == "MT":
                    _, l, n = op
                    u, hg = n // 2, n % 2
                    wait(sp_, a_dve, b, len(a_by_dve), a_dve_no[op])
                    for r, src in ((96, nm_hi), (97, nm_lo)):
                        dst = qst[r:r + 1, u, 4 * hg:4 * hg + 4, :]
                        sp_.dma_start(dst.bitcast(F32), src).then_inc(rows_in, 16)

            def expert_op(op, b):
                if op[0] == "W2" and op[2] == GT - 1:
                    g = op[1]
                    wait(sp_, f_dve, b, NFD, f_dve_no[op])
                    sp_.dma_start(out[b].rearrange("(t p) d -> p t d", p=P)[:, g * GT:(g + 1) * GT, :],
                                  x1[:, g * GT:(g + 1) * GT, :]).then_inc(out_done, 16)

            streams(sp_.Fori, lambda ba, bf: walk(attn_op, expert_op, ba, bf))
            sp_.wait_ge(out_done, 16 * B * G)

        @block.gpsimd
        def _(pool):
            gp = nc.gpsimd
            gp.memset(ident[:, :], 0.0).then_inc(s_prep_pool, 1)
            gp.memset(ones[:, :], 1.0).then_inc(s_prep_pool, 1)
            gp.memset(mhalf[:, :], -0.5).then_inc(s_prep_pool, 1)
            gp.memset(half[:, :, :], 0.5).then_inc(s_prep_pool, 1)
            gp.memset(mone[:, :], -1.0).then_inc(s_prep_pool, 1)
            gp.memset(lgp[:, :, :], SENTINEL).then_inc(s_prep_pool, 1)
            gp.memset(m8[:, :, :], SENTINEL).then_inc(s_prep_pool, 1)
            pool.wait_ge(s_prep_pool, 7)
            gp.affine_select(out=ident[:, :], in_=ident[:, :], compare_op=ALU.not_equal, fill=1.0,
                             base=0, pattern=[[-1, P]], channel_multiplier=1).then_inc(s_prep_pool, 1)
            seltmp = x1[0:C3, 3, 0:E1]
            gp.memset(seltmp, 0.0).then_inc(s_prep_pool, 1)
            pool.wait_ge(s_prep_pool, 9)
            gp.affine_select(out=seltmp, in_=seltmp, compare_op=ALU.not_equal, fill=1.0,
                             base=0, pattern=[[-1, E1]], channel_multiplier=1).then_inc(s_prep_pool, 1)
            pool.wait_ge(s_prep_pool, 10)
            gp.affine_select(out=seltmp, in_=seltmp, compare_op=ALU.not_equal, fill=1.0,
                             base=-E1, pattern=[[-1, E1]], channel_multiplier=1).then_inc(s_prep_pool, 1)
            pool.wait_ge(s_prep_pool, 11)
            gp.tensor_copy(sel[:, :], seltmp).then_inc(s_prep_pool, 1)
            for col, val in ((E, 1.0), (E1 + E, 0.0), (2 * E1 + E, 1.0)):
                gp.tensor_scalar(cst[:, :, col:col + 1], half[:, :, 0:1], 2.0 * val, None, ALU.mult)\
                    .then_inc(s_prep_pool, 1)

            def attn_op(op, b):
                if op == ("L1a",):
                    wait(pool, ag1, b, LT0, LT0, apart=True)
                    gp.tensor_scalar(rs1[:, :], mv1[:, :, 1], LN_EPS, None, ALU.add).then_inc(rs1_add, 1)
                    wait(pool, rs1_add, b, 1, 1)
                    gp.tensor_tensor(rs1[:, :], rs1[:, :], mhalf[:, 0:LT0], ALU.pow).then_inc(rs1_pow, 1)
                if op == ("NORM", NL - 1, 0):
                    wait(pool, xres_in, b, 16, 16)
                    if isinstance(b, int) and b == 0:
                        pool.wait_ge(s_prep_dve, N_DVE_PREP)
                    gp.tensor_tensor(xres[:, :, :], xres[:, :, :],
                                     bass.AP(tensor=brow[:, :].tensor, offset=brow[:, :].offset,
                                             ap=[brow[:, :].ap[0], [0, TT], [1, D]]),
                                     ALU.add).then_inc(xb_done, 1)
                if op[0] == "NORM":
                    _, l, n = op
                    u, hg = n // 2, n % 2
                    cu = levels[l].unit_len(u)
                    wait(pool, on_hi, b, NN, norm_no[op])
                    gp.tensor_tensor(xt_lo[:, hg, u * BANK:u * BANK + cu], o_n[:, 0:cu],
                                     xt_hi[:, hg, u * BANK:u * BANK + cu].bitcast(F32), ALU.subtract)\
                        .then_inc(on_lo, 1)

            def expert_op(op, b):
                g = op[1]
                if op[0] == "F1":
                    wait(pool, ag2, b, G * GT, (g + 1) * GT, apart=True)
                    gp.tensor_scalar(rs2[:, :], mv2[:, :, 1], LN_EPS, None, ALU.add).then_inc(rs2_add, 1)
                    wait(pool, rs2_add, b, G, g + 1)
                    gp.tensor_tensor(rs2[:, :], rs2[:, :], mhalf[:, 0:GT], ALU.pow).then_inc(rs2_pow, 1)
                if op[0] == "CW":
                    wait(pool, sp_c, b, G * N_SP, (g + 1) * N_SP)
                    gp.tensor_tensor(cw[:, 0, :, :], sp[:, 5, :, :], half[:, :, :], ALU.pow).then_inc(cw_c, 1)
                    wait(pool, cw_c, b, G * 5, g * 5 + 1)
                    wait(pool, mask_done, b, G, g + 1)
                    gp.tensor_tensor(cw[:, 1, :, :], cw[:, 0, :, :], mask[:, :, :], ALU.mult).then_inc(cw_c, 1)
                    wait(pool, cw_c, b, G * 5, g * 5 + 2, apart=True)
                    gp.tensor_copy(cst[:, :, 0:E], cw[:, 1, :, :]).then_inc(cw_c, 1)
                    gp.tensor_copy(cst[:, :, 2 * E1:2 * E1 + E], cw[:, 1, :, :]).then_inc(cw_c, 1)
                    wait(pool, cw_c, b, G * 5, g * 5 + 4)
                    gp.tensor_tensor(cst[:, :, E1:E1 + E], cw[:, 1, :, :], cst[:, :, 0:E].bitcast(F32),
                                     ALU.subtract).then_inc(cw_c, 1)

            streams(pool.Fori, lambda ba, bf: walk(attn_op, expert_op, ba, bf))

        N_PE_PREP = 2 * 2 * 2 + 2 * 1 + 2 * 1 + 1
        @block.scalar
        def _(act):
            ac = nc.scalar
            act.wait_ge(s_w, ALL_LOADS)
            n = [0]
            ac.activation(wl_hi[:, 0, :, :], win_st[0], ACT.Copy).then_inc(s_prep_act, 1)
            ac.activation(w1_hi[:, :, :], w1_st, ACT.Copy).then_inc(s_prep_act, 1)
            ac.activation(wo_hi[:, :, :], woutT_st[2], ACT.Copy).then_inc(s_prep_act, 1)
            ac.activation(wr_hi[:, :, :], wr_st, ACT.Copy).then_inc(s_prep_act, 1)
            ac.activation(b1h[:, :], b1c[:, :], ACT.Copy, scale=0.5).then_inc(s_prep_act, 1)
            k = 0
            for l in (1, 2):
                for m in range(2):
                    for c0, cn in ((0, 512), (512, 256)):
                        bk = a_bank[k % 2]
                        act.wait_ge(s_prep_pe, prep_pe_no[("C", l, m, c0)])
                        ac.activation(wl_hi[:, l, m, c0:c0 + cn], bk[:, 0:cn], ACT.Copy).then_inc(s_prep_act, 1)
                        k += 1

            def attn_op(op, b):
                kind = op[0]
                if kind in ("T1", "K", "Q", "V"):
                    i = a_index[op]
                    bk = a_bank[i % 2]
                    wait(act, a_ready, b, NA, i + 1)
                if kind == "T1":
                    ac.activation(xt_hi[:, op[1], 0:LT0 * P], bk[:, 0:LT0 * P], ACT.Copy).then_inc(hi_done, 1)
                if kind == "K":
                    _, l, hg, c = op
                    c0, cn = levels[l].key_chunks()[c]
                    ac.activation(kpack[:, 0, hg, c0:c0 + cn].bitcast(F32R), bk[:, 0:cn], ACT.Identity,
                                  bias=bcol[:, l, 2 + hg:3 + hg]).then_inc(hi_done, 1)
                if kind == "Q":
                    _, l, hg, u = op
                    cn = len(levels[l].units[u]) * levels[l].width
                    ac.activation(qpack[:, 0, u, hg, 0:cn].bitcast(F32R), bk[:, 0:cn],
                                  ACT.Identity, bias=bcol[:, l, hg:hg + 1]).then_inc(hi_done, 1)
                if kind == "V":
                    _, l, v = op
                    nv = min(2, levels[l].vtiles - v)
                    ac.activation(v_sb[:, v:v + nv, :], bk[:, 0:nv * D].rearrange("p (v d) -> p v d", v=nv),
                                  ACT.Copy).then_inc(a_act, 1)
                if kind == "ST":
                    _, l, nn, j, i = op
                    lev = levels[l]
                    w, kt = lev.steps(nn // 2)[j]
                    k, step = st_no[op], pv_no[("PV", l, nn, j)]
                    gs = heads_of(l, i)
                    qv = lev.queries(w)
                    src = st_bank[(k - 1) % 2][:, :].rearrange("p (g q) -> p g q", q=lev.width)[:, :, 0:qv]
                    dst = probs[:, (step - 1) % 2, :].rearrange("p (g q) -> p g q", g=4)[:, gs[0]:gs[-1] + 1, 0:qv]
                    wait(act, st_ready, b, NST, k)
                    wait(act, pv_done, b, NPV, step - 2)
                    ac.activation(dst, src, ACT.Exp, scale=SCALE).then_inc(exp_done, 1)

            def expert_op(op, b):
                g = op[1]
                if op[0] == "T2":
                    i = f_index[op]
                    wait(act, f_ready, b, NF, i + 1)
                    ac.activation(x2_hi[:, :, :], f_bank[i % 2][:, :].rearrange("p (k n) -> p k n", k=KD),
                                  ACT.Copy).then_inc(x2hi_done, 1)
                if op[0] == "LG":
                    i = f_index[op]
                    wait(act, f_ready, b, NF, i + 1)
                    ac.activation(lgt, f_bank[i % 2][0:E, 0:GN], ACT.Identity, bias=ebc[:, 0:1])\
                        .then_inc(f_act, 1)
                if op[0] == "CW":
                    wait(act, f_dve, b, NFD, f_dve_no[("LT", g)])
                    ac.activation(sp[:, 0, :, :], lgp[:, :, 0:E], ACT.Abs).then_inc(abs_done, 1)
                    wait(act, abs_done, b, G, g + 1)
                    ac.activation(sp[:, 1, :, :], sp[:, 0, :, :], ACT.Exp, scale=-1.0).then_inc(e_done, 1)
                if op[0] == "W1":
                    p = op[2]
                    es = range(2 * p, min(2 * p + 2, E1))
                    i, ic = f_index[op], f_index[("CB",) + op[1:]]
                    wait(act, f_ready, b, NF, ic + 1)
                    ac.activation(hs[:, es[0]:es[-1] + 1, :],
                                  f_bank[ic % 2][:, 0:len(es) * GN].rearrange("p (e n) -> p e n", n=GN),
                                  ACT.Copy).then_inc(f_act, 1)
                    wait(act, f_ready, b, NF, i + 1)
                    wait(act, f_dve, b, NFD, f_dve_no[op] - 2)
                    for j, e in enumerate(range(2 * p, min(2 * p + 2, E1))):
                        ac.activation(th[:, p % 2, j, :], f_bank[i % 2][:, j * GN:(j + 1) * GN], ACT.Tanh,
                                      bias=b1h[:, e:e + 1], scale=0.5).then_inc(th_done, 1)

            ac.preload_act_table_set(EXP_TANH)
            streams(act.Fori, lambda ba, bf: walk(attn_op, expert_op, ba, bf))

        @block.vector
        def _(dve):
            ve = nc.vector
            dve.wait_ge(s_w, ALL_LOADS)
            dve.wait_ge(s_prep_act, 4)
            ve.tensor_tensor(wl_lo[:, 0, :, :], win_st[0], wl_hi[:, 0, :, :].bitcast(F32), ALU.subtract)\
                .then_inc(s_prep_dve, 1)
            ve.tensor_tensor(w1_lo[:, :, :], w1_st, w1_hi[:, :, :].bitcast(F32), ALU.subtract)\
                .then_inc(s_prep_dve, 1)
            ve.tensor_tensor(wo_lo[:, :, :], woutT_st[2], wo_hi[:, :, :].bitcast(F32), ALU.subtract)\
                .then_inc(s_prep_dve, 1)
            ve.tensor_tensor(wr_lo[:, :, :], wr_st, wr_hi[:, :, :].bitcast(F32), ALU.subtract)\
                .then_inc(s_prep_dve, 1)
            ve.tensor_scalar(w2_sb[:, :, :], w2_sb[:, :, :], 0.5, None, ALU.mult).then_inc(s_prep_dve, 1)
            ve.tensor_copy(bcol[:, 0, :], bins_st[:, 0, :]).then_inc(s_prep_dve, 1)
            ve.tensor_copy(b2_hi.bitcast(F32R), b2_stg).then_inc(s_b2, 1)
            dve.wait_ge(s_b2, 1)
            ve.tensor_tensor(b2_lo.bitcast(F32R), b2_stg, b2_hi, ALU.subtract).then_inc(s_b2, 1)
            done = 6
            k = 0
            for l in (1, 2):
                dve.wait_ge(s_prep_pe, prep_pe_no[("t", l)])
                ve.tensor_tensor(t0c[:, l, :], f_bank[0][:, 0:2], bouts_st[:, l - 1, :], ALU.add)\
                    .then_inc(s_prep_dve, 1)
                done += 1
                dve.wait_ge(s_prep_pe, prep_pe_no[("b", l)])
                ve.tensor_tensor(bcol[:, l, :], f_bank[1][:, 0:6], bins_st[:, l, :], ALU.add)\
                    .then_inc(s_prep_dve, 1)
                done += 1
                for m in range(2):
                    for c0, cn in ((0, 512), (512, 256)):
                        dve.wait_ge(s_prep_act, 5 + k + 1)
                        ve.tensor_tensor(wl_lo[:, l, m, c0:c0 + cn], a_bank[k % 2][:, 0:cn],
                                         wl_hi[:, l, m, c0:c0 + cn].bitcast(F32), ALU.subtract)\
                            .then_inc(s_prep_dve, 1)
                        done += 1
                        k += 1
            dve.wait_ge(s_prep_dve, done)
            for kk in range(KD):
                ve.tensor_copy(colb[:, kk, :], spread(bcol[:, 2, 4 + kk:5 + kk], P))\
                    .then_inc(s_prep_dve, 1)
                done += 1
            dve.wait_ge(s_prep_pe, prep_pe_no[("r",)])
            ve.tensor_tensor(brow[:, :], f_bank[0][:, 0:D], bo2_st, ALU.add).then_inc(s_prep_dve, 1)
            dve.wait_ge(s_prep_dve, done + 1)
            ve.memset(stage1, 0.0).then_inc(s_prep_dve, 1)
            ve.memset(mx[:, :, :], 0.0).then_inc(s_prep_dve, 1)
            dve.wait_ge(s_prep_pool, 7)
            ve.tensor_scalar(kst[96:98, :, :].rearrange("p h n -> p (h n)"),
                             spread(mone[96:98, 0:1], HEADS * MAXTOK), -1.0, None, ALU.mult)\
                .then_inc(s_prep_dve, 1)
            done += 4
            assert done == N_DVE_PREP

            def attn_op(op, b):
                kind = op[0]
                if kind == "L1a":
                    wait(dve, xln_in, b, 16, 16)
                    for t in range(LT0):
                        ve.bn_stats(st1[:, t, :], xln[:, t, :]).then_inc(bn1, 1)
                    wait(dve, bn1, b, LT0, LT0, apart=True)
                    for t in range(LT0):
                        ve.bn_aggr(mv1[:, t, :], st1[:, t, :]).then_inc(ag1, 1)
                if kind == "L1b":
                    wait(dve, ag1, b, LT0, LT0)
                    wait(dve, rs1_pow, b, 1, 1)
                    for t in range(LT0):
                        ve.tensor_scalar(xln[:, t, :], xln[:, t, :], mv1[:, t, 0:1], rs1[:, t:t + 1],
                                         ALU.subtract, ALU.mult).then_inc(xn1, 1)
                if kind in ("T1", "K", "Q"):
                    bk = a_bank[a_index[op] % 2]
                    wait(dve, hi_done, b, len(hi_ops), hi_no[op])
                if kind in ("S", "MT", "OP"):
                    bk = a_bank[a_index[op] % 2]
                    wait(dve, a_ready, b, NA, a_index[op] + 1)
                if kind == "T1":
                    ve.tensor_tensor(xt_lo[:, op[1], 0:LT0 * P], bk[:, 0:LT0 * P],
                                     xt_hi[:, op[1], 0:LT0 * P].bitcast(F32), ALU.subtract).then_inc(a_dve, 1)
                if kind == "K":
                    _, l, hg, c = op
                    c0, cn = levels[l].key_chunks()[c]
                    ve.scalar_tensor_tensor(kpack[:, 1, hg, c0:c0 + cn].bitcast(F32R), bk[:, 0:cn],
                                            bcol[:, l, 2 + hg:3 + hg], kpack[:, 0, hg, c0:c0 + cn],
                                            ALU.add, ALU.subtract).then_inc(a_dve, 1)
                if kind == "Q":
                    _, l, hg, u = op
                    cn = len(levels[l].units[u]) * levels[l].width
                    ve.scalar_tensor_tensor(qpack[:, 1, u, hg, 0:cn].bitcast(F32R), bk[:, 0:cn],
                                            bcol[:, l, hg:hg + 1], qpack[:, 0, u, hg, 0:cn],
                                            ALU.add, ALU.subtract).then_inc(a_dve, 1)
                if kind == "S":
                    _, l, n, j, i = op
                    gs = heads_of(l, i)
                    ve.tensor_reduce(mx[:, n % 2, 4 * gs[0] + j:4 * gs[-1] + j + 1:4],
                                     bk[:, :].rearrange("p (g k) -> p g k", g=len(gs)), AX_X, ALU.max)\
                        .then_inc(a_dve, 1)
                if kind == "MT":
                    wait(dve, rows_in, b, 32 * NM, 32 * (mt_no[op] - 1))
                    ve.tensor_scalar(nm_hi.bitcast(F32R), bk[0:16, 0:P], -1.0, None, ALU.mult).then_inc(nmh_done, 1)
                    wait(dve, nmh_done, b, NM, mt_no[op])
                    ve.scalar_tensor_tensor(nm_lo.bitcast(F32R), bk[0:16, 0:P], -1.0, nm_hi,
                                            ALU.mult, ALU.subtract).then_inc(a_dve, 1)
                if kind == "NORM":
                    _, l, n = op
                    u, hg = n // 2, n % 2
                    cu = levels[l].unit_len(u)
                    wait(dve, pv_done, b, NPV, pv_no[("PV", l, n, len(levels[l].steps(u)) - 1)])
                    wait(dve, on_lo, b, NN, norm_no[op] - 1)
                    c3, nb = 3 * (norm_no[op] - 1), cu // DH
                    ve.transpose(o_n[:, 0:cu].bitcast(U32), sum_bank[:, 0:cu].bitcast(U32)).then_inc(rinv_c, 1)
                    wait(dve, rinv_c, b, 3 * NN, c3 + 1)
                    ve.reciprocal(rcol[:, 0:nb], o_n[:, 0:cu:DH]).then_inc(rinv_c, 1)
                    wait(dve, rinv_c, b, 3 * NN, c3 + 2)
                    ve.transpose(rinv[:, 0:cu].bitcast(U32),
                                 bass.AP(tensor=rcol[:, :].tensor, offset=rcol[:, :].offset,
                                         ap=[rcol[:, :].ap[0], [1, nb], [0, DH]]).bitcast(U32))\
                        .then_inc(rinv_c, 1)
                    wait(dve, rinv_c, b, 3 * NN, c3 + 3)
                    ve.tensor_tensor(o_n[:, 0:cu], o_bank[:, 0:cu], rinv[:, 0:cu], ALU.mult).then_inc(on_done, 1)
                    wait(dve, on_done, b, NN, norm_no[op])
                    ve.tensor_copy(xt_hi[:, hg, u * BANK:u * BANK + cu], o_n[:, 0:cu]).then_inc(on_hi, 1)
                if kind == "OP":
                    t = op[1]
                    if t == 0:
                        wait(dve, xb_done, b, 1, 1)
                        wait(dve, out_done, b, 16 * G, 0)
                    ve.tensor_tensor(x1[:, t:t + 2, :], bk[:, :].rearrange("p (t d) -> p t d", t=2),
                                     xres[:, t:t + 2, :], ALU.add).then_inc(a_dve, 1)

            def expert_op(op, b):
                g = op[1]
                if op[0] == "F1":
                    wait(dve, a_dve, b, len(a_by_dve), len(a_by_dve))
                    for t in range(GT):
                        ve.bn_stats(st2[:, t, :], x1[:, g * GT + t, :]).then_inc(bn2, 1)
                    wait(dve, bn2, b, G * GT, (g + 1) * GT, apart=True)
                    for t in range(GT):
                        ve.bn_aggr(mv2[:, t, :], st2[:, t, :]).then_inc(ag2, 1)
                if op[0] == "FN":
                    wait(dve, ag2, b, G * GT, (g + 1) * GT)
                    wait(dve, rs2_pow, b, G, g + 1)
                    for t in range(GT):
                        ve.tensor_scalar(xn2[:, t, :], x1[:, g * GT + t, :], mv2[:, t, 0:1], rs2[:, t:t + 1],
                                         ALU.subtract, ALU.mult).then_inc(xn2_done, 1)
                if op[0] == "T2":
                    i = f_index[op]
                    wait(dve, x2hi_done, b, G, g + 1)
                    ve.tensor_tensor(x2_lo[:, :, :], f_bank[i % 2][:, :].rearrange("p (k n) -> p k n", k=KD),
                                     x2_hi[:, :, :].bitcast(F32), ALU.subtract).then_inc(f_dve, 1)
                if op[0] == "LT":
                    i = f_index[op]
                    wait(dve, f_ready, b, NF, i + 1)
                    ve.tensor_copy(lgp[:, :, 0:E], f_bank[i % 2][:, 0:GT * E].rearrange("p (t e) -> p t e", t=GT))\
                        .then_inc(f_dve, 1)
                if op[0] == "TP":
                    wait(dve, f_dve, b, NFD, f_dve_no[("LT", g)], apart=True)
                    base = g * N_TOP
                    for t in range(GT):
                        ve.max(m8a[:, t, :], lgp[:, t, :]).then_inc(top_c, 1)
                    wait(dve, top_c, b, G * N_TOP, base + 2)
                    ve.tensor_copy(m8[:, :, 0:2], m8a[:, :, 0:2]).then_inc(top_c, 1)
                    wait(dve, top_c, b, G * N_TOP, base + 3, apart=True)
                    for t in range(GT):
                        ve.match_replace(rep[:, t, :], m8[:, t, :], lgp[:, t, :], -SENTINEL).then_inc(top_c, 1)
                    wait(dve, top_c, b, G * N_TOP, base + 5)
                    ve.tensor_tensor(mask[:, :, :], rep[:, :, 0:E], lgp[:, :, 0:E], ALU.not_equal)\
                        .then_inc(mask_done, 1)
                if op[0] == "CW":
                    base = g * N_SP
                    e, den, zz, z2, acc = (sp[:, k, :, :] for k in (1, 2, 3, 4, 5))
                    c = [0]

                    def link(ins):
                        c[0] += 1
                        ins.then_inc(sp_c, 1)
                        if c[0] < N_SP:
                            wait(dve, sp_c, b, G * N_SP, base + c[0])

                    wait(dve, e_done, b, G, g + 1)
                    link(ve.tensor_scalar(den, e, 2.0, None, ALU.add))
                    link(ve.reciprocal(den, den))
                    link(ve.scalar_tensor_tensor(zz, e, 2.0, den, ALU.mult, ALU.mult))
                    link(ve.scalar_tensor_tensor(z2, zz, 0.25, zz, ALU.mult, ALU.mult))
                    link(ve.tensor_scalar(acc, z2, 1.0 / 15, None, ALU.mult))
                    for k in LOG1P_TERMS:
                        link(ve.scalar_tensor_tensor(acc, acc, 1.0 / k, z2, ALU.add, ALU.mult))
                    link(ve.scalar_tensor_tensor(acc, acc, 1.0, zz, ALU.add, ALU.mult))
                    link(ve.scalar_tensor_tensor(acc, lgp[:, :, 0:E], 0.0, acc, ALU.max, ALU.add))
                    assert c[0] == N_SP
                if op[0] == "CT":
                    i = f_index[op]
                    wait(dve, f_ready, b, NF, i + 1)
                    ve.tensor_copy(ct[:, :], f_bank[i % 2][0:C3, 0:GN]).then_inc(f_dve, 1)
                if op[0] == "W1":
                    p = op[2]
                    es = range(2 * p, min(2 * p + 2, E1))
                    i = f_index[op]
                    wait(dve, th_done, b, G * E1, g * E1 + es[-1] + 1)
                    wait(dve, f_act, b, NFA, f_act_no[("CB",) + op[1:]])
                    ve.scalar_tensor_tensor(th[:, p % 2, 0:len(es), :], th[:, p % 2, 0:len(es), :], 1.0,
                                            hs[:, es[0]:es[-1] + 1, :],
                                            ALU.add, ALU.mult).then_inc(t1_done, 1)
                    wait(dve, t1_done, b, G * PAIRS, g * PAIRS + p + 1)
                    for j, e in enumerate(es):
                        last = ve.scalar_tensor_tensor(hs[:, e, :], f_bank[i % 2][:, j * GN:(j + 1) * GN],
                                                       b1c[:, e:e + 1], th[:, p % 2, j, :], ALU.add, ALU.mult)
                    last.then_inc(f_dve, 1)
                if op[0] == "W2":
                    i = f_index[op]
                    wait(dve, f_ready, b, NF, i + 1)
                    t = g * GT + op[2]
                    ve.tensor_tensor(x1[:, t, :], f_bank[i % 2][:, 0:D], x1[:, t, :], ALU.add).then_inc(f_dve, 1)

            streams(dve.Fori, lambda ba, bf: walk(attn_op, expert_op, ba, bf))

        @block.tensor
        def _(pe):
            te = nc.tensor
            pe.wait_ge(s_w, ALL_LOADS)
            for l in (1, 2):
                bin_prev, dn = (bins_st[:, 0, :], 6) if l == 1 else (bcol[:, 1, :], 8)
                wi = win_st[1] if l == 1 else win2_st
                if l == 2:
                    pe.wait_ge(s_prep_dve, 6 + 2 + 4)
                for m in range(2):
                    for k in range(KD):
                        last = te.matmul(f_bank[0][:, m:m + 1], woutT_st[l - 1][:, k, m * P:(m + 1) * P],
                                         bin_prev[:, 4 + k:5 + k], start=(k == 0), stop=(k == KD - 1))
                last.then_inc(s_prep_pe, 1)
                pe.wait_ge(s_prep_dve, {1: 7, 2: 13}[l])
                for m in range(6):
                    for k in range(KD):
                        last = te.matmul(f_bank[1][:, m:m + 1], wi[:, k, m * P:(m + 1) * P],
                                         t0c[:, l, k:k + 1], start=(k == 0), stop=(k == KD - 1))
                last.then_inc(s_prep_pe, 1)
                cc = (l - 1) * 4
                for m in range(2):
                    for c0, cn in ((0, 512), (512, 256)):
                        if cc >= 2:
                            pe.wait_ge(s_prep_dve, prep_dve_c[cc - 2])
                        for k in range(KD):
                            last = te.matmul(a_bank[cc % 2][:, 0:cn], wout_st[l - 1][:, k, m * P:(m + 1) * P],
                                             wi[:, k, c0:c0 + cn], start=(k == 0), stop=(k == KD - 1))
                        last.then_inc(s_prep_pe, 1)
                        cc += 1
            pe.wait_ge(s_prep_dve, N_DVE_PREP - 4)
            for k in range(KD):
                last = te.matmul(f_bank[0][:, 0:D], colb[:, k, :], woutT_st[2][:, k, :],
                                 start=(k == 0), stop=(k == KD - 1))
            last.then_inc(s_prep_pe, 1)
            pe.wait_ge(s_prep_dve, N_DVE_PREP)
            pe.wait_ge(s_prep_pool, 15)
            pe.wait_ge(s_b2, 34)

            def free_a(b, i):
                j = i - 2
                bb = b
                if j < 0:
                    j += NA
                    bb = b - 1
                if isinstance(bb, int) and bb < 0:
                    return
                o = a_items[j]
                if o in a_act_no:
                    wait(pe, a_act, bb, len(a_by_act), a_act_no[o])
                else:
                    wait(pe, a_dve, bb, len(a_by_dve), a_dve_no[o])

            def free_f(b, i):
                j = i - 2
                bb = b
                if j < 0:
                    j += NF
                    bb = b - 1
                if isinstance(bb, int) and bb < 0:
                    return
                o = f_items[j]
                if o in f_act_no:
                    wait(pe, f_act, bb, NFA, f_act_no[o])
                else:
                    wait(pe, f_dve, bb, NFD, f_dve_no[o])

            def three_pass(dst, lh, ll, rh, rl):
                n = 0
                for k in range(KD):
                    for a, c in ((lh, rh), (lh, rl), (ll, rh)):
                        last = te.matmul(dst, a(k), c(k), start=(n == 0), stop=(n == 3 * KD - 1))
                        n += 1
                return last

            def attn_op(op, b):
                kind = op[0]
                if kind in A_KINDS:
                    i = a_index[op]
                    bk = a_bank[i % 2]
                    free_a(b, i)
                if kind == "T1":
                    wait(pe, xn1, b, LT0, LT0)
                    for t in range(LT0):
                        last = te.transpose(bk[:, t * P:(t + 1) * P], xln[:, t, op[1] * P:(op[1] + 1) * P],
                                            ident[:, :])
                    last.then_inc(a_ready, 1)
                if kind in ("K", "Q", "V") and op[2] == 0 and (kind == "K" and op[3] == 0):
                    if op[1] == 0:
                        wait(pe, a_dve, b, len(a_by_dve), 2)
                    else:
                        wait(pe, on_lo, b, NN, 4 * op[1])
                if kind == "K":
                    _, l, hg, c = op
                    c0, cn = levels[l].key_chunks()[c]
                    cols = slice((2 + hg) * P, (3 + hg) * P)
                    three_pass(bk[:, 0:cn], lambda k: wl_hi[:, l, k, cols], lambda k: wl_lo[:, l, k, cols],
                               lambda k: xt_hi[:, k, c0:c0 + cn], lambda k: xt_lo[:, k, c0:c0 + cn])\
                        .then_inc(a_ready, 1)
                if kind == "Q":
                    _, l, hg, u = op
                    lev = levels[l]
                    nw = len(lev.units[u])
                    tok = lev.units[u][0] * lev.stride
                    cols = slice(hg * P, (hg + 1) * P)

                    def windows(t, k):
                        a = t[:, k, tok:tok + lev.width]
                        return bass.AP(tensor=a.tensor, offset=a.offset,
                                       ap=[a.ap[0], [lev.stride, nw], [1, lev.width]])

                    three_pass(bk[:, 0:nw * lev.width].rearrange("p (w q) -> p w q", w=nw),
                               lambda k: wl_hi[:, l, k, cols], lambda k: wl_lo[:, l, k, cols],
                               lambda k: windows(xt_hi, k), lambda k: windows(xt_lo, k)).then_inc(a_ready, 1)
                if kind == "V":
                    _, l, v = op
                    lev = levels[l]
                    for j in range(min(2, lev.vtiles - v)):
                        w, kt = divmod(v + j, lev.ktiles)
                        tok = w * lev.stride + kt * P
                        last = three_pass(bk[:, j * D:(j + 1) * D],
                                          lambda k: xt_hi[:, k, tok:tok + P], lambda k: xt_lo[:, k, tok:tok + P],
                                          lambda k: wl_hi[:, l, k, 2 * D:3 * D], lambda k: wl_lo[:, l, k, 2 * D:3 * D])
                    last.then_inc(a_ready, 1)
                if kind == "S":
                    _, l, n, j, i_ = op
                    lev = levels[l]
                    u, hg = n // 2, n % 2
                    if (n, j, i_) == (0, 0, 0):
                        wait(pe, stack_k, b, NL * STACK, (l + 1) * STACK)
                        wait(pe, stack_q, b, NL * STACK, (l + 1) * STACK)
                    pos = u * BANK + j * P
                    tok = pos // lev.width * lev.stride
                    for c, g in enumerate(heads_of(l, i_)):
                        h = 4 * hg + g
                        last = te.matmul(bk[:, c * lev.width:(c + 1) * lev.width], qst[0:96, u, h, j * P:(j + 1) * P],
                                         kst[0:96, h, tok:tok + lev.width], start=True, stop=True)
                    last.then_inc(a_ready, 1)
                if kind == "MT":
                    _, l, n = op
                    js = len(levels[l].steps(n // 2))
                    wait(pe, a_dve, b, len(a_by_dve), a_dve_no[("S", l, n, js - 1, levels[l].items - 1)])
                    te.transpose(bk[0:16, 0:P], mx[:, n % 2, :], ident[:, :]).then_inc(a_ready, 1)
                if kind == "ST":
                    _, l, n, j, i_ = op
                    lev = levels[l]
                    u, hg = n // 2, n % 2
                    w, kt = lev.steps(u)[j]
                    k = st_no[op]
                    if (j, i_) == (0, 0):
                        wait(pe, rows_in, b, 32 * NM, 32 * mt_no[("MT", l, n)])
                    wait(pe, exp_done, b, NST, k - 2)
                    tok = w * lev.stride + kt * P
                    for c, g in enumerate(heads_of(l, i_)):
                        h = 4 * hg + g
                        last = te.matmul(st_bank[(k - 1) % 2][:, c * lev.width:(c + 1) * lev.width],
                                         kst[:, h, tok:tok + P],
                                         qst[:, u, h, w * lev.width - u * BANK:(w + 1) * lev.width - u * BANK],
                                         start=True, stop=True)
                    last.then_inc(st_ready, 1)
                if kind == "PV":
                    _, l, n, j = op
                    lev = levels[l]
                    u, hg = n // 2, n % 2
                    w, kt = lev.steps(u)[j]
                    step = pv_no[op]
                    qv = lev.queries(w)
                    col = w * lev.width - u * BANK
                    wait(pe, exp_done, b, NST, st_no[("ST", l, n, j, lev.items - 1)])
                    if op == ("PV", l, n, 0):
                        wait(pe, on_done, b, NN, norm_no[("NORM", l, n)] - 1)
                        if n == 0:
                            wait(pe, a_act, b, len(a_by_act),
                                 a_act_no[[o for o in a_by_act if o[1] == l][-1]])
                    pr = probs[:, (step - 1) % 2, :].rearrange("p (g q) -> p g q", g=4)
                    for dst, lhs in ((o_bank, None), (sum_bank, ones_b)):
                        for g in range(4):
                            h = 4 * hg + g
                            vt = w * lev.ktiles + kt
                            last = te.matmul(dst[32 * g:32 * g + 32, col:col + qv],
                                             v_sb[:, vt, 32 * h:32 * h + 32] if lhs is None else lhs,
                                             pr[:, g, 0:qv], start=(kt == 0), stop=(kt == lev.ktiles - 1))
                    last.then_inc(pv_done, 1)
                if kind == "OP":
                    t0 = op[1]
                    if t0 == 0:
                        wait(pe, on_lo, b, NN, NN)
                    for j in range(2):
                        tok = (t0 + j) * P
                        last = three_pass(bk[:, j * D:(j + 1) * D],
                                          lambda k: xt_hi[:, k, tok:tok + P], lambda k: xt_lo[:, k, tok:tok + P],
                                          lambda k: wo_hi[:, k, :], lambda k: wo_lo[:, k, :])
                    last.then_inc(a_ready, 1)

            def expert_op(op, b):
                g = op[1]
                if op not in f_index:
                    return
                if op[0] == "W1":
                    p = op[2]
                    es = range(2 * p, min(2 * p + 2, E1))
                    if p == 0:
                        wait(pe, f_dve, b, NFD, f_dve_no[("CT", g)])
                    ic = f_index[("CB",) + op[1:]]
                    free_f(b, ic)
                    for j, e in enumerate(es):
                        last = te.matmul(f_bank[ic % 2][:, j * GN:(j + 1) * GN], spread(sel[:, e:e + 1], P), ct[:, :],
                                         start=True, stop=True)
                    last.then_inc(f_ready, 1)
                i = f_index[op]
                bk = f_bank[i % 2]
                free_f(b, i)
                if op[0] == "T2":
                    wait(pe, xn2_done, b, G * GT, (g + 1) * GT)
                    for k in range(KD):
                        for t in range(GT):
                            last = te.transpose(bk[:, k * GN + t * P:k * GN + (t + 1) * P],
                                                xn2[:, t, k * P:(k + 1) * P], ident[:, :])
                    last.then_inc(f_ready, 1)
                if op[0] == "LG":
                    wait(pe, f_dve, b, NFD, f_dve_no[("T2", g)])
                    three_pass(bk[0:E, 0:GN], lambda k: wr_hi[:, k, :], lambda k: wr_lo[:, k, :],
                               lambda k: x2_hi[:, k, :], lambda k: x2_lo[:, k, :]).then_inc(f_ready, 1)
                if op[0] == "LT":
                    wait(pe, f_act, b, NFA, f_act_no[("LG", g)], apart=True)
                    for t in range(GT):
                        last = te.transpose(bk[:, t * E:(t + 1) * E], lgt[:, t * P:(t + 1) * P], ident[0:E, 0:E])
                    last.then_inc(f_ready, 1)
                if op[0] == "CT":
                    wait(pe, cw_c, b, G * 5, (g + 1) * 5)
                    for t in range(GT):
                        last = te.transpose(bk[0:C3, t * P:(t + 1) * P], cst[:, t, :].bitcast(F32), ident[:, :])
                    last.then_inc(f_ready, 1)
                if op[0] == "W1":
                    for j, e in enumerate(es):
                        cols = slice(e * H, (e + 1) * H)
                        last = three_pass(bk[:, j * GN:(j + 1) * GN],
                                          lambda k: w1_hi[:, k, cols], lambda k: w1_lo[:, k, cols],
                                          lambda k: x2_hi[:, k, :], lambda k: x2_lo[:, k, :])
                    last.then_inc(f_ready, 1)
                if op[0] == "W2":
                    wait(pe, f_dve, b, NFD, f_dve_no[("W1", g, PAIRS - 1)])
                    t = op[2]
                    for e in range(E1):
                        te.matmul(bk[:, 0:D], hs[:, e, t * P:(t + 1) * P], w2_sb[:, e, :],
                                  start=(e == 0), stop=False)
                    last = te.matmul(bk[:, 0:D], ct[:, t * P:(t + 1) * P], b2_st[:, :], start=False, stop=True)
                    last.then_inc(f_ready, 1)

            streams(pe.Fori, lambda ba, bf: walk(attn_op, expert_op, ba, bf))


prep_pe_no, prep_dve_c = {}, []
for _l in (1, 2):
    prep_pe_no[("t", _l)] = len(prep_pe_no) + 1
    prep_pe_no[("b", _l)] = len(prep_pe_no) + 1
    for _m in range(2):
        for _c in (0, 512):
            prep_pe_no[("C", _l, _m, _c)] = len(prep_pe_no) + 1
            prep_dve_c.append(6 + 2 * _l + len(prep_dve_c) + 1)
prep_pe_no[("r",)] = len(prep_pe_no) + 1
N_DVE_PREP = 6 + 12 + 2 + 1 + 3


def kernel(**inputs):
    import numpy as np
    import concourse.bacc as bacc
    from concourse.bass_utils import run_bass_kernel_spmd as run

    nc = bacc.Bacc("TRN2", target_bir_lowering=False, num_devices=1, dynamic_dma_scratch_size=1024)
    arrays = {}

    def dram(name, a):
        a = np.ascontiguousarray(a)
        arrays[name] = a
        return nc.dram_tensor(name, a.shape, mybir.dt.from_np(a.dtype), kind="ExternalInput").ap()

    a = {k: np.asarray(v) for k, v in inputs.items()}
    x = a["L0_attn_x"]
    args = [
        dram("x", x),
        [dram(f"winT{l}", a[f"L0_attn_Win{l}"].T) for l in range(3)],
        dram("wout0", a["L0_attn_Wout0"]),
        dram("wout1", a["L0_attn_Wout1"]),
        [dram(f"woutT{l}", a[f"L0_attn_Wout{l}"].T) for l in range(3)],
        [dram(f"bin{l}", a[f"L0_attn_bin{l}"].reshape(-1, P).T) for l in range(3)],
        [dram(f"bout{l}", a[f"L0_attn_bout{l}"].reshape(-1, P).T) for l in range(2)]
        + [dram("bout2", a["L0_attn_bout2"])],
        dram("wrT", a["L0_ffn_routing_W"].T),
        dram("ebias", a["L0_ffn_expert_bias"]),
        dram("sw1", a["L0_ffn_sW1"]), dram("sb1", a["L0_ffn_sb1"]),
        dram("sw2", a["L0_ffn_sW2"]), dram("sb2", a["L0_ffn_sb2"]),
        dram("rw1", a["L0_ffn_rW1"]), dram("rb1T", a["L0_ffn_rb1"].T),
        dram("rw2", a["L0_ffn_rW2"]), dram("rb2", a["L0_ffn_rb2"]),
        nc.dram_tensor("out", x.shape, F32, kind="ExternalOutput").ap(),
    ]
    block_kernel(nc, *args)
    r = run(nc, [arrays], core_ids=[0])
    return r.results[0]["out"]
```

```python
from contextlib import ExitStack

import concourse.bass as bass
from concourse import mybir
from concourse.alu_op_type import AluOpType as ALU

F32 = mybir.dt.float32
F32R = mybir.dt.float32r
U32 = mybir.dt.uint32
ACT = mybir.ActivationFunctionType
AX_X = mybir.AxisListType.X

P = 128
BANK = 512
LN_EPS = 1e-5
OVERLAP = 64
SENTINEL = -3.0e38
EXP_TANH = "exp_and_others"
W_STEP, W_NORM, W_SMAX, W_DENSE, W_STACK, W_LEVEL = (1, 0.5, 0.15), 2, (0.3, 0.4, 0.4), 0.4, 6, 5
W2_PARTS = 3
LAG = 2
LOG1P_TERMS = (13, 11, 9, 7, 5, 3)


class Level:

    def __init__(self, width, out_len):
        self.width = width
        self.stride = width - OVERLAP
        self.windows = -(-out_len // width)
        self.out_len = out_len
        self.tokens = (self.windows - 1) * self.stride + width
        self.ktiles = width // P
        self.heads_per_item = BANK // width
        self.items = 4 // self.heads_per_item
        self.per_unit = BANK // width
        self.units = [list(range(u, min(u + self.per_unit, self.windows)))
                      for u in range(0, self.windows, self.per_unit)]
        self.vtiles = self.windows * self.ktiles

    def queries(self, w):
        return min(self.width, self.out_len - w * self.width)

    def unit_len(self, u):
        return sum(self.queries(w) for w in self.units[u])

    def steps(self, u):
        return [(w, kt) for w in self.units[u] for kt in range(self.ktiles)]

    def key_chunks(self):
        return [(c, min(BANK, self.tokens - c)) for c in range(0, self.tokens, BANK)]


def make_levels(seq, width0, n):
    widths = [width0 << i for i in range(n)]
    out_len, levels = seq, []
    for w in reversed(widths):
        lev = Level(w, out_len)
        levels.append(lev)
        out_len = lev.tokens
    return levels[::-1]


def attention_plan(levels, out_tiles):
    plan = [("T1", kt) for kt in range(2)] + [("HOOK", 1)]
    for l, lev in enumerate(levels):
        def dense(items):
            for it in items:
                plan.extend([it, ("HOOK", W_DENSE)])

        keys = [[("K", l, hg, c) for c in range(len(lev.key_chunks()))] for hg in range(2)]
        queries = [[("Q", l, hg, u) for u in range(2)] for hg in range(2)]
        dense(keys[0])
        dense(queries[0])
        dense(queries[1])
        dense([("V", l, v) for v in range(0, lev.vtiles, 2)])
        dense(keys[1])
        plan.append(("HOOK", W_STACK))
        if l == len(levels) - 1:
            plan.append(("L1",))

        def smax(n):
            return [[("S", l, n, j, i) for i in range(lev.items)] for j in range(len(lev.steps(n % 2)))]

        def probs(n):
            return [[("ST", l, n, j, i) for i in range(lev.items)] for j in range(len(lev.steps(n % 2)))]

        for j, items in enumerate(smax(0)):
            for it in items:
                plan += [it, ("HOOK", W_SMAX[l])]
        for j, items in enumerate(smax(1)):
            for it in items:
                plan += [it, ("HOOK", W_SMAX[l])]
            if j == 0:
                plan.append(("MT", l, 0))
        owed, cut = [], 0
        for n in range(4):
            ahead = smax(n + 2) if n < 2 else []
            for j, items in enumerate(probs(n)):
                both = [[a] for a in items]
                for k, a in enumerate(ahead[j] if j < len(ahead) else []):
                    both[k].append(a)
                half = (len(both) + 1) // 2
                for k, some in enumerate(both):
                    if k == half:
                        plan += owed[:cut]
                    if k:
                        plan.append(("HOOK", W_STEP[l]))
                    plan += some
                plan += owed[cut:] if len(both) > half else owed
                owed, cut = [("PS", l, n, j), ("PV", l, n, j)], 1
                if j == len(lev.steps(n % 2)) - 1:
                    owed, cut = [owed[0], ("INV", l, n), owed[1], ("NORM", l, n)], 2
                if j == 0 and n < 3:
                    plan.append(("MT", l, n + 1))
                plan.append(("HOOK", W_NORM if n and j == 0 else W_STEP[l]))
                if l == len(levels) - 1 and n == 1:
                    plan += {0: [("L1a",)], 2: [("L1b",)]}.get(j, [])
        plan += owed
        plan.append(("HOOK", W_LEVEL))
    for t in range(0, out_tiles, 2):
        plan.append(("OP", t))
    return plan


def expert_plan(groups, pairs, experts):
    def router(g, kinds):
        return [(k, g) for k in kinds]

    tail = ["LT", "TP", "CW"] + ["GAP"] * 2
    plan = router(0, ["F1", "GAP", "FN", "T2", "GAP", "LG"] + tail + ["GAP"] * 2 + ["CT"])
    for g in range(groups):
        more = g + 1 < groups
        for p in range(pairs):
            plan.append(("CB", g, p))
            plan += [("W1", g, e) for e in range(2 * p, min(2 * p + 2, experts))]
            if more and p in (1, 3):
                plan += router(g + 1, ["F1" if p == 1 else "FN"])
        plan += router(g + 1, ["T2", "GAP", "LG"]) if more else []
        plan += [("W2", g, 0, part) for part in range(W2_PARTS)]
        plan += router(g + 1, tail) if more else []
        plan += [("W2", g, 1, part) for part in range(W2_PARTS)]
        plan += router(g + 1, ["GAP", "CT"]) if more else []
    return plan


COST = dict(F1=0, FN=0, T2=0.5, LG=0.7, LT=0.2, TP=0, CW=0, GAP=0, CT=0.3, CB=0.3, W1=0.65, W2=1.3)
LATENCY = {("F1", "GAP"): 2, ("GAP", "FN"): 2, ("FN", "T2"): 1.5, ("T2", "GAP"): 2, ("GAP", "LG"): 2,
           ("LG", "LT"): 1.5, ("LG", "W2"): 0, ("LT", "TP"): 0.5, ("CW", "GAP"): 4, ("GAP", "GAP"): 4,
           ("GAP", "CT"): 4, ("CT", "CB"): 1, ("W1", "W1"): 0.3, ("W1", "W2"): 2.5, ("TP", "CW"): 0.5}


def place_tasks(tasks, hooks):
    scale = sum(COST[t[0]] for t in tasks) / sum(hooks)

    def price(room, some):
        load = sum(COST[t[0]] for t in some)
        stall = sum(LATENCY.get((a[0], c[0]), 0) for a, c in zip(some, some[1:]))
        return (load - room * scale) ** 2 + 2.0 * stall

    best = {0: (0.0, None)}
    trail = []
    for room in hooks:
        new = {}
        for i, (v, _) in best.items():
            for j in range(i, min(i + 6, len(tasks)) + 1):
                w = v + price(room, tasks[i:j])
                if j not in new or w < new[j][0]:
                    new[j] = (w, i)
        trail.append(new)
        best = new
    j, out_ = len(tasks), []
    for new in reversed(trail):
        i = new[j][1]
        out_.append([t for t in tasks[i:j] if t[0] != "GAP"])
        j = i
    return out_[::-1]


def merged(attn, at_hook):
    steps, k = [], 0
    for op in attn:
        if op[0] == "HOOK":
            steps += [("expert", task, n == len(at_hook[k]) - 1) for n, task in enumerate(at_hook[k])]
            steps.append(("hook",))
            k += 1
        else:
            steps.append(("attention", op))
    return steps


def late(steps, kinds, pace, lag):
    steps, i = list(steps), 0
    while i < len(steps):
        st = steps[i]
        if st[0] == "expert" and st[2] and st[1][0] in kinds:
            j, seen = i + 2, 0
            while j < len(steps) and seen < lag and steps[j][0] == "attention" and steps[j][1][0] not in ("OP", "NORM"):
                seen += steps[j][1][0] in pace
                j += 1
            steps[i:j] = steps[i + 1:j] + [("expert", st[1], False)]
        else:
            i += 1
    return steps


def block_kernel(nc, x, winT, wout0, wout1, woutT, bins, bouts, wrT, ebias,
                 sw1, sb1, sw2, sb2, rw1, rb1T, rw2, rb2, out):
    B, L, D = x.shape
    H, E = rb1T.shape
    HEADS, DH = 8, 32
    SCALE = float(DH) ** -0.5
    KD = D // P
    TT = L // P
    E1 = E + 1
    C3 = 3 * E1
    GT = 2
    G = TT // GT
    GN = GT * P
    PAIRS = (E1 + 1) // 2
    levels = make_levels(L, 128, 3)
    assert KD == 2 and HEADS == 8 and H == P and all(len(v.units) == 2 for v in levels)
    LT0 = levels[0].tokens // P

    attn = attention_plan(levels, TT)
    tasks = expert_plan(G, PAIRS, E1)
    experts = [task for task in tasks if task[0] != "GAP"]
    steps = merged(attn, place_tasks(tasks, [op[1] for op in attn if op[0] == "HOOK"]))
    vector_steps = late(steps, ("W1", "W2", "T2"), ("K", "Q", "S"), LAG)
    sync_steps = late(steps, ("W2",), (), 1)

    A_KINDS = ("T1", "K", "Q", "V", "S", "MT", "OP")
    a_items = [op for op in attn if op[0] in A_KINDS]
    a_index = {op: i for i, op in enumerate(a_items)}
    NA = len(a_items)
    a_by_act = [op for op in a_items if op[0] == "V"]
    a_by_dve = [op for op in a_items if op[0] != "V"]
    a_act_no = {op: i + 1 for i, op in enumerate(a_by_act)}
    a_dve_no = {op: i + 1 for i, op in enumerate(a_by_dve)}
    hi_ops = [op for op in a_items if op[0] in ("T1", "K", "Q")]
    hi_no = {op: i + 1 for i, op in enumerate(hi_ops)}
    st_items = [op for op in attn if op[0] == "ST"]
    st_no = {op: i + 1 for i, op in enumerate(st_items)}
    NST = len(st_items)
    pv_ops = [op for op in attn if op[0] == "PV"]
    pv_no = {op: i + 1 for i, op in enumerate(pv_ops)}
    NPV = len(pv_ops)
    norm_no = {op: i + 1 for i, op in enumerate([op for op in attn if op[0] == "NORM"])}
    NN = len(norm_no)
    mt_no = {op: i + 1 for i, op in enumerate([op for op in attn if op[0] == "MT"])}
    NM = len(mt_no)
    f_items = []
    for op in experts:
        if op[0] in ("T2", "LG", "LT", "CT", "CB", "W1") or op[0] == "W2" and op[3] == 0:
            f_items.append(op[:3])
    f_index = {op: i for i, op in enumerate(f_items)}
    NF = len(f_items)
    f_act_no = {op: i + 1 for i, op in enumerate([op for op in f_items if op[0] in ("LG", "CB")])}
    f_dve_no = {op: i + 1 for i, op in enumerate([op for op in f_items if op[0] not in ("LG", "CB")])}
    NFA, NFD = len(f_act_no), len(f_dve_no)
    assert NA % 2 == 0 and NST % 2 == 0 and NPV % 2 == 0 and NF % 2 == 0
    STACK = 12 * 16
    NL = len(levels)
    MAXPOS = max(v.windows * v.width for v in levels)
    MAXTOK = max(v.tokens for v in levels)

    with ExitStack() as ctx:
        def sb(name, shape, dt=F32):
            return ctx.enter_context(nc.sbuf_tensor(name, shape, dt))

        def sem(name):
            return ctx.enter_context(nc.semaphore(name))

        wl_hi = sb("wl_hi", [P, NL, KD, 3 * D], F32R)
        wl_lo = sb("wl_lo", [P, NL, KD, 3 * D], F32R)
        wo_hi = sb("wo_hi", [P, KD, D], F32R)
        wo_lo = sb("wo_lo", [P, KD, D], F32R)
        w1_hi = sb("w1_hi", [P, KD, E1 * H], F32R)
        w1_lo = sb("w1_lo", [P, KD, E1 * H], F32R)
        w2_sb = sb("w2_sb", [P, E1, D])
        wr_hi = sb("wr_hi", [P, KD, E], F32R)
        wr_lo = sb("wr_lo", [P, KD, E], F32R)
        b2_st = sb("b2_st", [C3, D], F32R)
        sel = sb("sel", [C3, E1], F32R)
        b1c = sb("b1c", [P, E1])
        b1h = sb("b1h", [P, E1])
        ebc = sb("ebc", [E, 1])
        bcol = sb("bcol", [P, NL, 6])
        t0c = sb("t0c", [P, NL, KD])
        ident = sb("ident", [P, P])
        ones = sb("ones", [P, DH])
        brow = sb("brow", [P, D])
        xt_hi = sb("xt_hi", [P, KD, MAXPOS], F32R)
        xt_lo = sb("xt_lo", [P, KD, MAXPOS], F32R)
        kpack = sb("kpack", [P, 2, 2, MAXPOS])
        qpack = sb("qpack", [P, 2, 2, 2, BANK])
        kst = sb("kst", [98, HEADS, MAXTOK], F32R)
        qst = sb("qst", [98, 2, HEADS, BANK], F32R)
        v_sb = sb("v_sb", [P, 8, D])
        xln = sb("xln", [P, LT0, D])
        x1 = sb("x1", [P, TT, D])
        mx = sb("mx", [P, 2, 16])
        rows = sb("rows", [P, 2 * P])
        st1 = sb("st1", [P, LT0, 6])
        mv1 = sb("mv1", [P, LT0, 2])
        rs1 = sb("rs1", [P, LT0])
        st2 = sb("st2", [P, GT, 6])
        mv2 = sb("mv2", [P, GT, 2])
        rs2 = sb("rs2", [P, GT])
        mhalf = sb("mhalf", [P, 4])
        half = sb("half", [P, GT, E])
        mone = sb("mone", [P, 1])
        rcol = sb("rcol", [P, BANK // DH])
        xn2 = sb("xn2", [P, GT, D])
        x2_hi = sb("x2_hi", [P, KD, GN], F32R)
        x2_lo = sb("x2_lo", [P, KD, GN], F32R)
        lgt = rows[0:E, 0:GN]
        nm_hi = rows[32:48, 0:P]
        nm_lo = rows[32:48, P:2 * P]
        lgp = sb("lgp", [P, GT, 16])
        rep = sb("rep", [P, GT, 16])
        m8a = sb("m8a", [P, GT, 8])
        m8 = sb("m8", [P, GT, 8])
        mask = sb("mask", [P, GT, E])
        sp = sb("sp", [P, 6, GT, E])
        cw = sb("cw", [P, 2, GT, E])
        cst = sb("cst", [P, GT, C3], F32R)
        ct = sb("ct", [C3, GN], F32R)
        th = sb("th", [P, 4, GN])
        hs = sb("hs", [P, E1, GN])
        probs = qpack[:, :, :, :, :].rearrange("p a u b c -> p (a u b c)").rearrange("p (s n) -> p s n", s=2)
        kflat = kpack[:, :, :, :].rearrange("p a b c -> p (a b c)")
        xres = kflat[:, 0:TT * D].rearrange("p (t d) -> p t d", t=TT)
        rinv = kflat[:, TT * D:TT * D + BANK]
        o_n = kflat[:, TT * D + BANK:TT * D + 2 * BANK]
        ones_b = ones[:, :]

        def bank(name):
            return ctx.enter_context(nc.psum_tensor(name, [P, BANK], F32))

        a_bank = [bank("a0"), bank("a1")]
        st_bank = [bank("st0"), bank("st1b")]
        f_bank = [bank("f0"), bank("f1")]
        o_bank, sum_bank = bank("o"), bank("sum")

        s_w = sem("s_w")
        s_prep_pe, s_prep_act, s_prep_dve = sem("s_prep_pe"), sem("s_prep_act"), sem("s_prep_dve")
        s_prep_pool = sem("s_prep_pool")
        s_b2 = sem("s_b2")
        a_ready = sem("a_ready")
        a_act = sem("a_act")
        a_dve = sem("a_dve")
        hi_done = sem("hi_done")
        st_ready = sem("st_ready")
        exp_done = sem("exp_done")
        ps_done = sem("ps_done")
        pv_done = sem("pv_done")
        rinv_c = sem("rinv_c")
        on_done = sem("on_done")
        on_hi = sem("on_hi")
        on_lo = sem("on_lo")
        nmh_done = sem("nmh_done")
        stack_k = [sem("stack_k0"), sem("stack_k1")]
        stack_q = [sem("stack_q0"), sem("stack_q1")]
        rows_in = sem("rows_in")
        xln_in, xres_in = sem("xln_in"), sem("xres_in")
        xb_done = sem("xb_done")
        bn1, ag1, rs1_add, rs1_pow, xn1 = sem("bn1"), sem("ag1"), sem("rs1_add"), sem("rs1_pow"), sem("xn1")
        f_ready, f_act, f_dve = sem("f_ready"), sem("f_act"), sem("f_dve")
        bn2, ag2, rs2_add, rs2_pow, xn2_done = sem("bn2"), sem("ag2"), sem("rs2_add"), sem("rs2_pow"), sem("xn2_done")
        x2hi_done = sem("x2hi_done")
        top_c = sem("top_c")
        mask_done = sem("mask_done")
        abs_done, e_done = sem("abs_done"), sem("e_done")
        sp_c = sem("sp_c")
        cw_c = sem("cw_c")
        th_done = sem("th_done")
        t1_done = sem("t1_done")
        out_done = sem("out_done")
        passed = sem("passed")

        N_SP = len(LOG1P_TERMS) + 7
        N_TOP = 2 + 1 + 2

        def wait(eng, s, b, per_batch, n, apart=False):
            v = b * per_batch + n
            if not isinstance(v, int) or v > 0:
                eng.wait_ge(s, v)
            if apart and not isinstance(v, int):
                eng.sem_inc(passed, 1)

        def streams(engine_loop, body):
            body(0, None)
            body(1, 0)
            with engine_loop(2, B - 1) as i:
                body(i, i - 1)
            body(B - 1, B - 2)
            body(None, B - 1)

        def walk(steps, attn_op, expert_op, ba, bf):
            if isinstance(ba, int) and ba == 0:
                for op in (("L1",), ("L1a",), ("L1b",)):
                    attn_op(op, 0)
            for step in steps:
                if step[0] == "expert" and bf is not None:
                    expert_op(step[1], bf)
                if step[0] == "attention" and ba is not None:
                    op = step[1]
                    if op[0] not in ("L1", "L1a", "L1b"):
                        attn_op(op, ba)
                    elif not (isinstance(ba, int) and ba == B - 1):
                        attn_op(op, ba + 1)

        def spread(col, n):
            return bass.AP(tensor=col.tensor, offset=col.offset, ap=[col.ap[0], [0, n]])

        def heads_of(l, i):
            n = levels[l].heads_per_item
            return range(i * n, (i + 1) * n)

        stage0 = kpack[:, :, :, :].rearrange("p a b c -> p (a b c)")
        stage1 = qpack[:, :, :, :, :].rearrange("p a u b c -> p (a u b c)")
        win_st = [stage0[:, i * 2 * 768:(i + 1) * 2 * 768].rearrange("p (k n) -> p k n", k=2) for i in range(2)]
        wout_st = [stage0[:, 3072:3584].rearrange("p (k n) -> p k n", k=2),
                   stage0[:, 3584:4096].rearrange("p (k n) -> p k n", k=2)]
        win2_st = stage1[:, 0:1536].rearrange("p (k n) -> p k n", k=2)
        woutT_st = [stage1[:, 1536 + i * 512:2048 + i * 512].rearrange("p (k n) -> p k n", k=2) for i in range(3)]
        bins_st = stage1[:, 3072:3072 + 18].rearrange("p (l m) -> p l m", l=3)
        bouts_st = stage1[:, 3096:3096 + 6].rearrange("p (l m) -> p l m", l=3)
        wr_st = stage1[:, 3104:3120].rearrange("p (k n) -> p k n", k=2)
        bo2_st = stage1[:, 3120:3120 + 256]
        colb = stage1[:, 3376:3376 + 256].rearrange("p (k n) -> p k n", k=2)
        w1_st = hs[:, :, :].rearrange("p e n -> p (e n)").rearrange("p (k n) -> p k n", k=2)
        b2_stg = x1[0:C3, 0, :]
        b2_hi = x1[0:C3, 1, :]
        b2_lo = x1[0:C3, 2, :]
        N_W = 0

        block = ctx.enter_context(nc.Block())

        loads = [
            (win_st[0], winT[0].rearrange("(k p) n -> p k n", p=P)),
            (win_st[1], winT[1].rearrange("(k p) n -> p k n", p=P)),
            (win2_st, winT[2].rearrange("(k p) n -> p k n", p=P)),
            (wout_st[0], wout0.rearrange("(k p) n -> p k n", p=P)),
            (wout_st[1], wout1.rearrange("(k p) n -> p k n", p=P)),
            (woutT_st[0], woutT[0].rearrange("(k p) n -> p k n", p=P)),
            (woutT_st[1], woutT[1].rearrange("(k p) n -> p k n", p=P)),
            (woutT_st[2], woutT[2].rearrange("(k p) n -> p k n", p=P)),
            (bins_st[:, 0, :], bins[0]),
            (bins_st[:, 1, :], bins[1]),
            (bins_st[:, 2, :], bins[2]),
            (bouts_st[:, 0, :], bouts[0]),
            (bouts_st[:, 1, :], bouts[1]),
            (bo2_st, bass.AP(tensor=bouts[2].tensor, offset=bouts[2].offset, ap=[[0, P], [1, D]])),
            (wr_st, wrT.rearrange("(k p) n -> p k n", p=P)),
            (ebc[:, :], ebias.rearrange("(e a) -> e a", a=1)),
            (b1c[:, 0:E], rb1T),
            (b1c[:, E:E1], sb1.rearrange("(h a) -> h a", a=1)),
            (w2_sb[:, 0:E, :], rw2.rearrange("e h d -> h e d")),
            (w2_sb[:, E, :], sw2),
        ] + [
            (w1_st[:, k, 0:E * H].rearrange("p (e h) -> p e h", e=E),
             rw1.rearrange("e (k p) h -> k p e h", p=P)[k]) for k in range(KD)
        ] + [
            (w1_st[:, :, E * H:], sw1.rearrange("(k p) h -> p k h", p=P)),
        ] + [
            (b2_stg[r * E1:r * E1 + E, :], rb2) for r in range(3)
        ] + [
            (b2_stg[r * E1 + E:(r + 1) * E1, :], sb2.rearrange("(a n) -> a n", a=1)) for r in range(3)
        ]
        ALL_LOADS = 16 * len(loads)

        @block.sync
        def _(sp_):
            for dst, src in loads:
                sp_.dma_start(dst, src).then_inc(s_w, 16)
            sp_.wait_ge(s_b2, 2)
            sp_.dma_start(b2_st[0:2 * E1, :].bitcast(F32), b2_hi[0:2 * E1, :]).then_inc(s_b2, 16)
            sp_.dma_start(b2_st[2 * E1:C3, :].bitcast(F32), b2_lo[2 * E1:C3, :]).then_inc(s_b2, 16)

            def attn_op(op, b):
                kind = op[0]
                if kind == "L1":
                    wait(sp_, a_ready, b, NA, 2 - NA)
                    sp_.dma_start(xln[:, :, :], x[b][0:LT0 * P].rearrange("(t p) d -> p t d", p=P))\
                        .then_inc(xln_in, 16)
                if op == ("S", NL - 1, 1, 0, 0):
                    for hg in range(2):
                        wait(sp_, stack_k[hg], b, NL * STACK, NL * STACK)
                    sp_.dma_start(xres[:, :, :], x[b].rearrange("(t p) d -> p t d", p=P)).then_inc(xres_in, 16)
                if kind == "K" and op == [o for o in a_items if o[:3] == op[:3]][-1]:
                    wait(sp_, a_dve, b, len(a_by_dve), a_dve_no[op])
                    n, hg = levels[op[1]].tokens, op[2]
                    for r, part in enumerate((0, 0, 1)):
                        for g in range(4):
                            sp_.dma_start(kst[32 * r:32 * r + 32, 4 * hg + g, 0:n].bitcast(F32),
                                          kpack[32 * g:32 * g + 32, part, hg, 0:n]).then_inc(stack_k[hg], 16)
                if kind == "Q" and op == [o for o in a_items if o[:3] == op[:3]][-1]:
                    hg = op[2]
                    wait(sp_, a_dve, b, len(a_by_dve), a_dve_no[op])
                    for r, part in enumerate((0, 1, 0)):
                        for g in range(4):
                            sp_.dma_start(
                                qst[32 * r:32 * r + 32, :, 4 * hg + g, :].bitcast(F32),
                                qpack[32 * g:32 * g + 32, part, :, hg, :]).then_inc(stack_q[hg], 16)

            def expert_op(op, b):
                if op[0] == "W2" and op[2:] == (GT - 1, W2_PARTS - 1):
                    g = op[1]
                    wait(sp_, f_dve, b, NFD, f_dve_no[op[:3]])
                    sp_.dma_start(out[b].rearrange("(t p) d -> p t d", p=P)[:, g * GT:(g + 1) * GT, :],
                                  x1[:, g * GT:(g + 1) * GT, :]).then_inc(out_done, 16)

            streams(sp_.Fori, lambda ba, bf: walk(sync_steps, attn_op, expert_op, ba, bf))
            sp_.wait_ge(out_done, 16 * B * G)

        @block.gpsimd
        def _(pool):
            gp = nc.gpsimd
            gp.memset(ident[:, :], 0.0).then_inc(s_prep_pool, 1)
            gp.memset(ones[:, :], 1.0).then_inc(s_prep_pool, 1)
            gp.memset(mhalf[:, :], -0.5).then_inc(s_prep_pool, 1)
            gp.memset(half[:, :, :], 0.5).then_inc(s_prep_pool, 1)
            gp.memset(mone[:, :], -1.0).then_inc(s_prep_pool, 1)
            gp.memset(lgp[:, :, :], SENTINEL).then_inc(s_prep_pool, 1)
            gp.memset(m8[:, :, :], SENTINEL).then_inc(s_prep_pool, 1)
            pool.wait_ge(s_prep_pool, 7)
            gp.affine_select(out=ident[:, :], in_=ident[:, :], compare_op=ALU.not_equal, fill=1.0,
                             base=0, pattern=[[-1, P]], channel_multiplier=1).then_inc(s_prep_pool, 1)
            seltmp = x1[0:C3, 3, 0:E1]
            gp.memset(seltmp, 0.0).then_inc(s_prep_pool, 1)
            pool.wait_ge(s_prep_pool, 9)
            gp.affine_select(out=seltmp, in_=seltmp, compare_op=ALU.not_equal, fill=1.0,
                             base=0, pattern=[[-1, E1]], channel_multiplier=1).then_inc(s_prep_pool, 1)
            pool.wait_ge(s_prep_pool, 10)
            gp.affine_select(out=seltmp, in_=seltmp, compare_op=ALU.not_equal, fill=1.0,
                             base=-E1, pattern=[[-1, E1]], channel_multiplier=1).then_inc(s_prep_pool, 1)
            pool.wait_ge(s_prep_pool, 11)
            gp.tensor_copy(sel[:, :], seltmp).then_inc(s_prep_pool, 1)
            for col, val in ((E, 1.0), (E1 + E, 0.0), (2 * E1 + E, 1.0)):
                gp.tensor_scalar(cst[:, :, col:col + 1], half[:, :, 0:1], 2.0 * val, None, ALU.mult)\
                    .then_inc(s_prep_pool, 1)

            def attn_op(op, b):
                if op == ("L1a",):
                    wait(pool, ag1, b, LT0, LT0, apart=True)
                    gp.tensor_scalar(rs1[:, :], mv1[:, :, 1], LN_EPS, None, ALU.add).then_inc(rs1_add, 1)
                    wait(pool, rs1_add, b, 1, 1)
                    gp.tensor_tensor(rs1[:, :], rs1[:, :], mhalf[:, 0:LT0], ALU.pow).then_inc(rs1_pow, 1)
                if op == ("NORM", NL - 1, 0):
                    wait(pool, xres_in, b, 16, 16)
                    if isinstance(b, int) and b == 0:
                        pool.wait_ge(s_prep_dve, N_DVE_PREP)
                    gp.tensor_tensor(xres[:, :, :], xres[:, :, :],
                                     bass.AP(tensor=brow[:, :].tensor, offset=brow[:, :].offset,
                                             ap=[brow[:, :].ap[0], [0, TT], [1, D]]),
                                     ALU.add).then_inc(xb_done, 1)
                if op[0] == "NORM":
                    _, l, n = op
                    hg, u = n // 2, n % 2
                    cu = levels[l].unit_len(u)
                    wait(pool, on_hi, b, NN, norm_no[op])
                    gp.tensor_tensor(xt_lo[:, hg, u * BANK:u * BANK + cu], o_n[:, 0:cu],
                                     xt_hi[:, hg, u * BANK:u * BANK + cu].bitcast(F32), ALU.subtract)\
                        .then_inc(on_lo, 1)

            def expert_op(op, b):
                g = op[1]
                if op[0] == "F1":
                    wait(pool, ag2, b, G * GT, (g + 1) * GT, apart=True)
                    gp.tensor_scalar(rs2[:, :], mv2[:, :, 1], LN_EPS, None, ALU.add).then_inc(rs2_add, 1)
                    wait(pool, rs2_add, b, G, g + 1)
                    gp.tensor_tensor(rs2[:, :], rs2[:, :], mhalf[:, 0:GT], ALU.pow).then_inc(rs2_pow, 1)
                if op[0] == "CW":
                    wait(pool, sp_c, b, G * N_SP, (g + 1) * N_SP)
                    gp.tensor_tensor(cw[:, 0, :, :], sp[:, 5, :, :], half[:, :, :], ALU.pow).then_inc(cw_c, 1)
                    wait(pool, cw_c, b, G * 5, g * 5 + 1)
                    wait(pool, mask_done, b, G, g + 1)
                    gp.tensor_tensor(cw[:, 1, :, :], cw[:, 0, :, :], mask[:, :, :], ALU.mult).then_inc(cw_c, 1)
                    wait(pool, cw_c, b, G * 5, g * 5 + 2, apart=True)
                    gp.tensor_copy(cst[:, :, 0:E], cw[:, 1, :, :]).then_inc(cw_c, 1)
                    gp.tensor_copy(cst[:, :, 2 * E1:2 * E1 + E], cw[:, 1, :, :]).then_inc(cw_c, 1)
                    wait(pool, cw_c, b, G * 5, g * 5 + 4)
                    gp.tensor_tensor(cst[:, :, E1:E1 + E], cw[:, 1, :, :], cst[:, :, 0:E].bitcast(F32),
                                     ALU.subtract).then_inc(cw_c, 1)

            streams(pool.Fori, lambda ba, bf: walk(steps, attn_op, expert_op, ba, bf))

        N_PE_PREP = 2 * 2 * 2 + 2 * 1 + 2 * 1 + 1
        @block.scalar
        def _(act):
            ac = nc.scalar
            act.wait_ge(s_w, ALL_LOADS)
            n = [0]
            ac.activation(wl_hi[:, 0, :, :], win_st[0], ACT.Copy).then_inc(s_prep_act, 1)
            ac.activation(w1_hi[:, :, :], w1_st, ACT.Copy).then_inc(s_prep_act, 1)
            ac.activation(wo_hi[:, :, :], woutT_st[2], ACT.Copy).then_inc(s_prep_act, 1)
            ac.activation(wr_hi[:, :, :], wr_st, ACT.Copy).then_inc(s_prep_act, 1)
            ac.activation(b1h[:, :], b1c[:, :], ACT.Copy, scale=0.5).then_inc(s_prep_act, 1)
            k = 0
            for l in (1, 2):
                for m in range(2):
                    for c0, cn in ((0, 512), (512, 256)):
                        bk = a_bank[k % 2]
                        act.wait_ge(s_prep_pe, prep_pe_no[("C", l, m, c0)])
                        ac.activation(wl_hi[:, l, m, c0:c0 + cn], bk[:, 0:cn], ACT.Copy).then_inc(s_prep_act, 1)
                        k += 1

            def attn_op(op, b):
                kind = op[0]
                if kind in ("T1", "K", "Q", "V"):
                    i = a_index[op]
                    bk = a_bank[i % 2]
                    wait(act, a_ready, b, NA, i + 1)
                if kind == "T1":
                    ac.activation(xt_hi[:, op[1], 0:LT0 * P], bk[:, 0:LT0 * P], ACT.Copy).then_inc(hi_done, 1)
                if kind == "K":
                    _, l, hg, c = op
                    c0, cn = levels[l].key_chunks()[c]
                    ac.activation(kpack[:, 0, hg, c0:c0 + cn].bitcast(F32R), bk[:, 0:cn], ACT.Identity,
                                  bias=bcol[:, l, 2 + hg:3 + hg]).then_inc(hi_done, 1)
                if kind == "Q":
                    _, l, hg, u = op
                    cn = len(levels[l].units[u]) * levels[l].width
                    ac.activation(qpack[:, 0, u, hg, 0:cn].bitcast(F32R), bk[:, 0:cn],
                                  ACT.Identity, bias=bcol[:, l, hg:hg + 1]).then_inc(hi_done, 1)
                if kind == "V":
                    _, l, v = op
                    nv = min(2, levels[l].vtiles - v)
                    ac.activation(v_sb[:, v:v + nv, :], bk[:, 0:nv * D].rearrange("p (v d) -> p v d", v=nv),
                                  ACT.Copy).then_inc(a_act, 1)
                if kind == "MT":
                    _, l, n = op
                    hg, u = n // 2, n % 2
                    wait(act, a_dve, b, len(a_by_dve), a_dve_no[op])
                    for r, src in ((96, nm_hi), (97, nm_lo)):
                        dst = qst[r:r + 1, u, 4 * hg:4 * hg + 4, :]
                        act.dma_start(dst.bitcast(F32), src).then_inc(rows_in, 16)
                if kind == "ST":
                    _, l, nn, j, i = op
                    if (nn, j, i) == (0, 0, 0):
                        wait(act, stack_q[1], b, NL * STACK, (l + 1) * STACK)
                    lev = levels[l]
                    w, kt = lev.steps(nn % 2)[j]
                    k, step = st_no[op], pv_no[("PV", l, nn, j)]
                    gs = heads_of(l, i)
                    qv = lev.queries(w)
                    src = st_bank[(k - 1) % 2][:, :].rearrange("p (g q) -> p g q", q=lev.width)[:, :, 0:qv]
                    dst = probs[:, (step - 1) % 2, :].rearrange("p (g q) -> p g q", g=4)[:, gs[0]:gs[-1] + 1, 0:qv]
                    wait(act, st_ready, b, NST, k)
                    wait(act, pv_done, b, NPV, step - 2)
                    ac.activation(dst, src, ACT.Exp, scale=SCALE).then_inc(exp_done, 1)

            def expert_op(op, b):
                g = op[1]
                if op[0] == "T2":
                    i = f_index[op]
                    wait(act, f_ready, b, NF, i + 1)
                    ac.activation(x2_hi[:, :, :], f_bank[i % 2][:, :].rearrange("p (k n) -> p k n", k=KD),
                                  ACT.Copy).then_inc(x2hi_done, 1)
                if op[0] == "LG":
                    i = f_index[op]
                    wait(act, f_ready, b, NF, i + 1)
                    ac.activation(lgt, f_bank[i % 2][0:E, 0:GN], ACT.Identity, bias=ebc[:, 0:1])\
                        .then_inc(f_act, 1)
                if op[0] == "CW":
                    wait(act, f_dve, b, NFD, f_dve_no[("LT", g)])
                    ac.activation(sp[:, 0, :, :], lgp[:, :, 0:E], ACT.Abs).then_inc(abs_done, 1)
                    wait(act, abs_done, b, G, g + 1)
                    ac.activation(sp[:, 1, :, :], sp[:, 0, :, :], ACT.Exp, scale=-1.0).then_inc(e_done, 1)
                if op[0] == "CB":
                    i, e0 = f_index[op], 2 * op[2]
                    ne = min(2, E1 - e0)
                    wait(act, f_ready, b, NF, i + 1)
                    ac.activation(hs[:, e0:e0 + ne, :],
                                  f_bank[i % 2][:, 0:ne * GN].rearrange("p (e n) -> p e n", n=GN),
                                  ACT.Copy).then_inc(f_act, 1)
                if op[0] == "W1":
                    i, e = f_index[op], op[2]
                    wait(act, f_ready, b, NF, i + 1)
                    wait(act, f_dve, b, NFD, f_dve_no[op] - 4)
                    ac.activation(th[:, (g * E1 + e) % 4, :], f_bank[i % 2][:, 0:GN], ACT.Tanh,
                                  bias=b1h[:, e:e + 1], scale=0.5).then_inc(th_done, 1)

            ac.preload_act_table_set(EXP_TANH)
            streams(act.Fori, lambda ba, bf: walk(steps, attn_op, expert_op, ba, bf))

        @block.vector
        def _(dve):
            ve = nc.vector
            dve.wait_ge(s_w, ALL_LOADS)
            dve.wait_ge(s_prep_act, 4)
            ve.tensor_tensor(wl_lo[:, 0, :, :], win_st[0], wl_hi[:, 0, :, :].bitcast(F32), ALU.subtract)\
                .then_inc(s_prep_dve, 1)
            ve.tensor_tensor(w1_lo[:, :, :], w1_st, w1_hi[:, :, :].bitcast(F32), ALU.subtract)\
                .then_inc(s_prep_dve, 1)
            ve.tensor_tensor(wo_lo[:, :, :], woutT_st[2], wo_hi[:, :, :].bitcast(F32), ALU.subtract)\
                .then_inc(s_prep_dve, 1)
            ve.tensor_tensor(wr_lo[:, :, :], wr_st, wr_hi[:, :, :].bitcast(F32), ALU.subtract)\
                .then_inc(s_prep_dve, 1)
            ve.tensor_scalar(w2_sb[:, :, :], w2_sb[:, :, :], 0.5, None, ALU.mult).then_inc(s_prep_dve, 1)
            ve.tensor_copy(bcol[:, 0, :], bins_st[:, 0, :]).then_inc(s_prep_dve, 1)
            ve.tensor_copy(b2_hi.bitcast(F32R), b2_stg).then_inc(s_b2, 1)
            dve.wait_ge(s_b2, 1)
            ve.tensor_tensor(b2_lo.bitcast(F32R), b2_stg, b2_hi, ALU.subtract).then_inc(s_b2, 1)
            done = 6
            k = 0
            for l in (1, 2):
                dve.wait_ge(s_prep_pe, prep_pe_no[("t", l)])
                ve.tensor_tensor(t0c[:, l, :], f_bank[0][:, 0:2], bouts_st[:, l - 1, :], ALU.add)\
                    .then_inc(s_prep_dve, 1)
                done += 1
                dve.wait_ge(s_prep_pe, prep_pe_no[("b", l)])
                ve.tensor_tensor(bcol[:, l, :], f_bank[1][:, 0:6], bins_st[:, l, :], ALU.add)\
                    .then_inc(s_prep_dve, 1)
                done += 1
                for m in range(2):
                    for c0, cn in ((0, 512), (512, 256)):
                        dve.wait_ge(s_prep_act, 5 + k + 1)
                        ve.tensor_tensor(wl_lo[:, l, m, c0:c0 + cn], a_bank[k % 2][:, 0:cn],
                                         wl_hi[:, l, m, c0:c0 + cn].bitcast(F32), ALU.subtract)\
                            .then_inc(s_prep_dve, 1)
                        done += 1
                        k += 1
            dve.wait_ge(s_prep_dve, done)
            for kk in range(KD):
                ve.tensor_copy(colb[:, kk, :], spread(bcol[:, 2, 4 + kk:5 + kk], P))\
                    .then_inc(s_prep_dve, 1)
                done += 1
            dve.wait_ge(s_prep_pe, prep_pe_no[("r",)])
            ve.tensor_tensor(brow[:, :], f_bank[0][:, 0:D], bo2_st, ALU.add).then_inc(s_prep_dve, 1)
            dve.wait_ge(s_prep_dve, done + 1)
            ve.memset(stage1, 0.0).then_inc(s_prep_dve, 1)
            ve.memset(mx[:, :, :], 0.0).then_inc(s_prep_dve, 1)
            dve.wait_ge(s_prep_pool, 7)
            ve.tensor_scalar(kst[96:98, :, :].rearrange("p h n -> p (h n)"),
                             spread(mone[96:98, 0:1], HEADS * MAXTOK), -1.0, None, ALU.mult)\
                .then_inc(s_prep_dve, 1)
            done += 4
            assert done == N_DVE_PREP

            def attn_op(op, b):
                kind = op[0]
                if kind == "L1a":
                    wait(dve, xln_in, b, 16, 16)
                    for t in range(LT0):
                        ve.bn_stats(st1[:, t, :], xln[:, t, :]).then_inc(bn1, 1)
                    wait(dve, bn1, b, LT0, LT0, apart=True)
                    for t in range(LT0):
                        ve.bn_aggr(mv1[:, t, :], st1[:, t, :]).then_inc(ag1, 1)
                if kind == "L1b":
                    wait(dve, ag1, b, LT0, LT0)
                    wait(dve, rs1_pow, b, 1, 1)
                    for t in range(LT0):
                        ve.tensor_scalar(xln[:, t, :], xln[:, t, :], mv1[:, t, 0:1], rs1[:, t:t + 1],
                                         ALU.subtract, ALU.mult).then_inc(xn1, 1)
                if kind in ("T1", "K", "Q"):
                    bk = a_bank[a_index[op] % 2]
                    wait(dve, hi_done, b, len(hi_ops), hi_no[op])
                if kind in ("S", "MT", "OP"):
                    bk = a_bank[a_index[op] % 2]
                    wait(dve, a_ready, b, NA, a_index[op] + 1)
                if kind == "T1":
                    ve.tensor_tensor(xt_lo[:, op[1], 0:LT0 * P], bk[:, 0:LT0 * P],
                                     xt_hi[:, op[1], 0:LT0 * P].bitcast(F32), ALU.subtract).then_inc(a_dve, 1)
                if kind == "K":
                    _, l, hg, c = op
                    c0, cn = levels[l].key_chunks()[c]
                    ve.scalar_tensor_tensor(kpack[:, 1, hg, c0:c0 + cn].bitcast(F32R), bk[:, 0:cn],
                                            bcol[:, l, 2 + hg:3 + hg], kpack[:, 0, hg, c0:c0 + cn],
                                            ALU.add, ALU.subtract).then_inc(a_dve, 1)
                if kind == "Q":
                    _, l, hg, u = op
                    cn = len(levels[l].units[u]) * levels[l].width
                    ve.scalar_tensor_tensor(qpack[:, 1, u, hg, 0:cn].bitcast(F32R), bk[:, 0:cn],
                                            bcol[:, l, hg:hg + 1], qpack[:, 0, u, hg, 0:cn],
                                            ALU.add, ALU.subtract).then_inc(a_dve, 1)
                if kind == "S":
                    _, l, n, j, i = op
                    gs = heads_of(l, i)
                    ve.tensor_reduce(mx[:, n % 2, 4 * gs[0] + j:4 * gs[-1] + j + 1:4],
                                     bk[:, :].rearrange("p (g k) -> p g k", g=len(gs)), AX_X, ALU.max)\
                        .then_inc(a_dve, 1)
                if kind == "MT":
                    wait(dve, rows_in, b, 32 * NM, 32 * (mt_no[op] - 1))
                    ve.tensor_scalar(nm_hi.bitcast(F32R), bk[0:16, 0:P], -1.0, None, ALU.mult).then_inc(nmh_done, 1)
                    wait(dve, nmh_done, b, NM, mt_no[op])
                    ve.scalar_tensor_tensor(nm_lo.bitcast(F32R), bk[0:16, 0:P], -1.0, nm_hi,
                                            ALU.mult, ALU.subtract).then_inc(a_dve, 1)
                if kind == "INV":
                    _, l, n = op
                    hg, u = n // 2, n % 2
                    cu = levels[l].unit_len(u)
                    wait(dve, ps_done, b, NPV, pv_no[("PV", l, n, len(levels[l].steps(u)) - 1)])
                    wait(dve, on_lo, b, NN, norm_no[("NORM", l, n)] - 1)
                    k = norm_no[("NORM", l, n)]
                    c3, nb = 3 * (k - 1), cu // DH
                    ve.transpose(o_n[:, 0:cu].bitcast(U32), sum_bank[:, 0:cu].bitcast(U32)).then_inc(rinv_c, 1)
                    wait(dve, rinv_c, b, 3 * NN, c3 + 1)
                    ve.reciprocal(rcol[:, 0:nb], o_n[:, 0:cu:DH]).then_inc(rinv_c, 1)
                    wait(dve, rinv_c, b, 3 * NN, c3 + 2)
                    ve.transpose(rinv[:, 0:cu].bitcast(U32),
                                 bass.AP(tensor=rcol[:, :].tensor, offset=rcol[:, :].offset,
                                         ap=[rcol[:, :].ap[0], [1, nb], [0, DH]]).bitcast(U32))\
                        .then_inc(rinv_c, 1)
                if kind == "NORM":
                    _, l, n = op
                    hg, u = n // 2, n % 2
                    cu = levels[l].unit_len(u)
                    wait(dve, rinv_c, b, 3 * NN, 3 * norm_no[op])
                    wait(dve, pv_done, b, NPV, pv_no[("PV", l, n, len(levels[l].steps(u)) - 1)])
                    ve.tensor_tensor(o_n[:, 0:cu], o_bank[:, 0:cu], rinv[:, 0:cu], ALU.mult).then_inc(on_done, 1)
                    wait(dve, on_done, b, NN, norm_no[op])
                    ve.tensor_copy(xt_hi[:, hg, u * BANK:u * BANK + cu], o_n[:, 0:cu]).then_inc(on_hi, 1)
                if kind == "OP":
                    t = op[1]
                    if t == 0:
                        wait(dve, xb_done, b, 1, 1)
                        wait(dve, out_done, b, 16 * G, 0)
                    ve.tensor_tensor(x1[:, t:t + 2, :], bk[:, :].rearrange("p (t d) -> p t d", t=2),
                                     xres[:, t:t + 2, :], ALU.add).then_inc(a_dve, 1)

            def expert_op(op, b):
                g = op[1]
                if op[0] == "F1":
                    wait(dve, a_dve, b, len(a_by_dve), len(a_by_dve))
                    for t in range(GT):
                        ve.bn_stats(st2[:, t, :], x1[:, g * GT + t, :]).then_inc(bn2, 1)
                    wait(dve, bn2, b, G * GT, (g + 1) * GT, apart=True)
                    for t in range(GT):
                        ve.bn_aggr(mv2[:, t, :], st2[:, t, :]).then_inc(ag2, 1)
                if op[0] == "FN":
                    wait(dve, ag2, b, G * GT, (g + 1) * GT)
                    wait(dve, rs2_pow, b, G, g + 1)
                    for t in range(GT):
                        ve.tensor_scalar(xn2[:, t, :], x1[:, g * GT + t, :], mv2[:, t, 0:1], rs2[:, t:t + 1],
                                         ALU.subtract, ALU.mult).then_inc(xn2_done, 1)
                if op[0] == "T2":
                    i = f_index[op]
                    wait(dve, x2hi_done, b, G, g + 1)
                    ve.tensor_tensor(x2_lo[:, :, :], f_bank[i % 2][:, :].rearrange("p (k n) -> p k n", k=KD),
                                     x2_hi[:, :, :].bitcast(F32), ALU.subtract).then_inc(f_dve, 1)
                if op[0] == "LT":
                    i = f_index[op]
                    wait(dve, f_ready, b, NF, i + 1)
                    ve.tensor_copy(lgp[:, :, 0:E], f_bank[i % 2][:, 0:GT * E].rearrange("p (t e) -> p t e", t=GT))\
                        .then_inc(f_dve, 1)
                if op[0] == "TP":
                    wait(dve, f_dve, b, NFD, f_dve_no[("LT", g)], apart=True)
                    base = g * N_TOP
                    for t in range(GT):
                        ve.max(m8a[:, t, :], lgp[:, t, :]).then_inc(top_c, 1)
                    wait(dve, top_c, b, G * N_TOP, base + 2)
                    ve.tensor_copy(m8[:, :, 0:2], m8a[:, :, 0:2]).then_inc(top_c, 1)
                    wait(dve, top_c, b, G * N_TOP, base + 3, apart=True)
                    for t in range(GT):
                        ve.match_replace(rep[:, t, :], m8[:, t, :], lgp[:, t, :], -SENTINEL).then_inc(top_c, 1)
                    wait(dve, top_c, b, G * N_TOP, base + 5)
                    ve.tensor_tensor(mask[:, :, :], rep[:, :, 0:E], lgp[:, :, 0:E], ALU.not_equal)\
                        .then_inc(mask_done, 1)
                if op[0] == "CW":
                    base = g * N_SP
                    e, den, zz, z2, acc = (sp[:, k, :, :] for k in (1, 2, 3, 4, 5))
                    c = [0]

                    def link(ins):
                        c[0] += 1
                        ins.then_inc(sp_c, 1)
                        if c[0] < N_SP:
                            wait(dve, sp_c, b, G * N_SP, base + c[0])

                    wait(dve, e_done, b, G, g + 1)
                    link(ve.tensor_scalar(den, e, 2.0, None, ALU.add))
                    link(ve.reciprocal(den, den))
                    link(ve.scalar_tensor_tensor(zz, e, 2.0, den, ALU.mult, ALU.mult))
                    link(ve.scalar_tensor_tensor(z2, zz, 0.25, zz, ALU.mult, ALU.mult))
                    link(ve.tensor_scalar(acc, z2, 1.0 / 15, None, ALU.mult))
                    for k in LOG1P_TERMS:
                        link(ve.scalar_tensor_tensor(acc, acc, 1.0 / k, z2, ALU.add, ALU.mult))
                    link(ve.scalar_tensor_tensor(acc, acc, 1.0, zz, ALU.add, ALU.mult))
                    link(ve.scalar_tensor_tensor(acc, lgp[:, :, 0:E], 0.0, acc, ALU.max, ALU.add))
                    assert c[0] == N_SP
                if op[0] == "CT":
                    i = f_index[op]
                    wait(dve, f_ready, b, NF, i + 1)
                    ve.tensor_copy(ct[:, :], f_bank[i % 2][0:C3, 0:GN]).then_inc(f_dve, 1)
                if op[0] == "W1":
                    i, e = f_index[op], op[2]
                    tanh = th[:, (g * E1 + e) % 4, :]
                    wait(dve, th_done, b, G * E1, g * E1 + e + 1)
                    wait(dve, f_act, b, NFA, f_act_no[("CB", g, e // 2)])
                    ve.scalar_tensor_tensor(tanh, tanh, 1.0, hs[:, e, :], ALU.add, ALU.mult).then_inc(t1_done, 1)
                    wait(dve, t1_done, b, G * E1, g * E1 + e + 1)
                    ve.scalar_tensor_tensor(hs[:, e, :], f_bank[i % 2][:, 0:GN], b1c[:, e:e + 1], tanh,
                                            ALU.add, ALU.mult).then_inc(f_dve, 1)
                if op[0] == "W2" and op[3] == W2_PARTS - 1:
                    i = f_index[op[:3]]
                    wait(dve, f_ready, b, NF, i + 1)
                    t = g * GT + op[2]
                    ve.tensor_tensor(x1[:, t, :], f_bank[i % 2][:, 0:D], x1[:, t, :], ALU.add).then_inc(f_dve, 1)

            streams(dve.Fori, lambda ba, bf: walk(vector_steps, attn_op, expert_op, ba, bf))

        @block.tensor
        def _(pe):
            te = nc.tensor
            pe.wait_ge(s_w, ALL_LOADS)
            for l in (1, 2):
                bin_prev, dn = (bins_st[:, 0, :], 6) if l == 1 else (bcol[:, 1, :], 8)
                wi = win_st[1] if l == 1 else win2_st
                if l == 2:
                    pe.wait_ge(s_prep_dve, 6 + 2 + 4)
                for m in range(2):
                    for k in range(KD):
                        last = te.matmul(f_bank[0][:, m:m + 1], woutT_st[l - 1][:, k, m * P:(m + 1) * P],
                                         bin_prev[:, 4 + k:5 + k], start=(k == 0), stop=(k == KD - 1))
                last.then_inc(s_prep_pe, 1)
                pe.wait_ge(s_prep_dve, {1: 7, 2: 13}[l])
                for m in range(6):
                    for k in range(KD):
                        last = te.matmul(f_bank[1][:, m:m + 1], wi[:, k, m * P:(m + 1) * P],
                                         t0c[:, l, k:k + 1], start=(k == 0), stop=(k == KD - 1))
                last.then_inc(s_prep_pe, 1)
                cc = (l - 1) * 4
                for m in range(2):
                    for c0, cn in ((0, 512), (512, 256)):
                        if cc >= 2:
                            pe.wait_ge(s_prep_dve, prep_dve_c[cc - 2])
                        for k in range(KD):
                            last = te.matmul(a_bank[cc % 2][:, 0:cn], wout_st[l - 1][:, k, m * P:(m + 1) * P],
                                             wi[:, k, c0:c0 + cn], start=(k == 0), stop=(k == KD - 1))
                        last.then_inc(s_prep_pe, 1)
                        cc += 1
            pe.wait_ge(s_prep_dve, N_DVE_PREP - 4)
            for k in range(KD):
                last = te.matmul(f_bank[0][:, 0:D], colb[:, k, :], woutT_st[2][:, k, :],
                                 start=(k == 0), stop=(k == KD - 1))
            last.then_inc(s_prep_pe, 1)
            pe.wait_ge(s_prep_dve, N_DVE_PREP)
            pe.wait_ge(s_prep_pool, 15)
            pe.wait_ge(s_b2, 34)

            def free_a(b, i):
                j = i - 2
                bb = b
                if j < 0:
                    j += NA
                    bb = b - 1
                if isinstance(bb, int) and bb < 0:
                    return
                o = a_items[j]
                if o in a_act_no:
                    wait(pe, a_act, bb, len(a_by_act), a_act_no[o])
                else:
                    wait(pe, a_dve, bb, len(a_by_dve), a_dve_no[o])

            def free_f(b, i):
                j = i - 2
                bb = b
                if j < 0:
                    j += NF
                    bb = b - 1
                if isinstance(bb, int) and bb < 0:
                    return
                o = f_items[j]
                if o in f_act_no:
                    wait(pe, f_act, bb, NFA, f_act_no[o])
                else:
                    wait(pe, f_dve, bb, NFD, f_dve_no[o])

            def three_pass(dst, lh, ll, rh, rl):
                n = 0
                for k in range(KD):
                    for a, c in ((lh, rh), (lh, rl), (ll, rh)):
                        last = te.matmul(dst, a(k), c(k), start=(n == 0), stop=(n == 3 * KD - 1))
                        n += 1
                return last

            def attn_op(op, b):
                kind = op[0]
                if kind in A_KINDS:
                    i = a_index[op]
                    bk = a_bank[i % 2]
                    free_a(b, i)
                if kind == "T1":
                    wait(pe, xn1, b, LT0, LT0)
                    for t in range(LT0):
                        last = te.transpose(bk[:, t * P:(t + 1) * P], xln[:, t, op[1] * P:(op[1] + 1) * P],
                                            ident[:, :])
                    last.then_inc(a_ready, 1)
                if kind in ("K", "Q", "V") and op[2] == 0 and (kind == "K" and op[3] == 0):
                    if op[1] == 0:
                        wait(pe, a_dve, b, len(a_by_dve), 2)
                    else:
                        wait(pe, on_lo, b, NN, 4 * op[1])
                if kind == "K":
                    _, l, hg, c = op
                    c0, cn = levels[l].key_chunks()[c]
                    cols = slice((2 + hg) * P, (3 + hg) * P)
                    three_pass(bk[:, 0:cn], lambda k: wl_hi[:, l, k, cols], lambda k: wl_lo[:, l, k, cols],
                               lambda k: xt_hi[:, k, c0:c0 + cn], lambda k: xt_lo[:, k, c0:c0 + cn])\
                        .then_inc(a_ready, 1)
                if kind == "Q":
                    _, l, hg, u = op
                    lev = levels[l]
                    nw = len(lev.units[u])
                    tok = lev.units[u][0] * lev.stride
                    cols = slice(hg * P, (hg + 1) * P)

                    def windows(t, k):
                        a = t[:, k, tok:tok + lev.width]
                        return bass.AP(tensor=a.tensor, offset=a.offset,
                                       ap=[a.ap[0], [lev.stride, nw], [1, lev.width]])

                    three_pass(bk[:, 0:nw * lev.width].rearrange("p (w q) -> p w q", w=nw),
                               lambda k: wl_hi[:, l, k, cols], lambda k: wl_lo[:, l, k, cols],
                               lambda k: windows(xt_hi, k), lambda k: windows(xt_lo, k)).then_inc(a_ready, 1)
                if kind == "V":
                    _, l, v = op
                    lev = levels[l]
                    for j in range(min(2, lev.vtiles - v)):
                        w, kt = divmod(v + j, lev.ktiles)
                        tok = w * lev.stride + kt * P
                        last = three_pass(bk[:, j * D:(j + 1) * D],
                                          lambda k: xt_hi[:, k, tok:tok + P], lambda k: xt_lo[:, k, tok:tok + P],
                                          lambda k: wl_hi[:, l, k, 2 * D:3 * D], lambda k: wl_lo[:, l, k, 2 * D:3 * D])
                    last.then_inc(a_ready, 1)
                if kind == "S":
                    _, l, n, j, i_ = op
                    lev = levels[l]
                    hg, u = n // 2, n % 2
                    if n % 2 == 0 and (j, i_) == (0, 0):
                        wait(pe, stack_k[hg], b, NL * STACK, (l + 1) * STACK)
                        wait(pe, stack_q[hg], b, NL * STACK, (l + 1) * STACK)
                    pos = u * BANK + j * P
                    tok = pos // lev.width * lev.stride
                    for c, g in enumerate(heads_of(l, i_)):
                        h = 4 * hg + g
                        last = te.matmul(bk[:, c * lev.width:(c + 1) * lev.width], qst[0:96, u, h, j * P:(j + 1) * P],
                                         kst[0:96, h, tok:tok + lev.width], start=True, stop=True)
                    last.then_inc(a_ready, 1)
                if kind == "MT":
                    _, l, n = op
                    js = len(levels[l].steps(n % 2))
                    wait(pe, a_dve, b, len(a_by_dve), a_dve_no[("S", l, n, js - 1, levels[l].items - 1)])
                    te.transpose(bk[0:16, 0:P], mx[:, n % 2, :], ident[:, :]).then_inc(a_ready, 1)
                if kind == "ST":
                    _, l, n, j, i_ = op
                    lev = levels[l]
                    hg, u = n // 2, n % 2
                    w, kt = lev.steps(u)[j]
                    k = st_no[op]
                    if (j, i_) == (0, 0):
                        wait(pe, rows_in, b, 32 * NM, 32 * mt_no[("MT", l, n)])
                    wait(pe, exp_done, b, NST, k - 2)
                    tok = w * lev.stride + kt * P
                    for c, g in enumerate(heads_of(l, i_)):
                        h = 4 * hg + g
                        last = te.matmul(st_bank[(k - 1) % 2][:, c * lev.width:(c + 1) * lev.width],
                                         kst[:, h, tok:tok + P],
                                         qst[:, u, h, w * lev.width - u * BANK:(w + 1) * lev.width - u * BANK],
                                         start=True, stop=True)
                    last.then_inc(st_ready, 1)
                if kind in ("PV", "PS"):
                    _, l, n, j = op
                    lev = levels[l]
                    hg, u = n // 2, n % 2
                    w, kt = lev.steps(u)[j]
                    step = pv_no[("PV", l, n, j)]
                    qv = lev.queries(w)
                    col = w * lev.width - u * BANK
                    wait(pe, exp_done, b, NST, st_no[("ST", l, n, j, lev.items - 1)])
                    if kind == "PS" and j == 0:
                        wait(pe, rinv_c, b, 3 * NN, 3 * (norm_no[("NORM", l, n)] - 2) + 1)
                    if kind == "PV" and j == 0:
                        wait(pe, on_done, b, NN, norm_no[("NORM", l, n)] - 1)
                        if n == 0:
                            wait(pe, a_act, b, len(a_by_act),
                                 a_act_no[[o for o in a_by_act if o[1] == l][-1]])
                    pr = probs[:, (step - 1) % 2, :].rearrange("p (g q) -> p g q", g=4)
                    dst = o_bank if kind == "PV" else sum_bank
                    for g in range(4):
                        h = 4 * hg + g
                        vt = w * lev.ktiles + kt
                        last = te.matmul(dst[32 * g:32 * g + 32, col:col + qv],
                                         v_sb[:, vt, 32 * h:32 * h + 32] if kind == "PV" else ones_b,
                                         pr[:, g, 0:qv], start=(kt == 0), stop=(kt == lev.ktiles - 1))
                    last.then_inc(pv_done if kind == "PV" else ps_done, 1)
                if kind == "OP":
                    t0 = op[1]
                    if t0 == 0:
                        wait(pe, on_lo, b, NN, NN)
                    for j in range(2):
                        tok = (t0 + j) * P
                        last = three_pass(bk[:, j * D:(j + 1) * D],
                                          lambda k: xt_hi[:, k, tok:tok + P], lambda k: xt_lo[:, k, tok:tok + P],
                                          lambda k: wo_hi[:, k, :], lambda k: wo_lo[:, k, :])
                    last.then_inc(a_ready, 1)

            def expert_op(op, b):
                g = op[1]
                if op[:3] not in f_index:
                    return
                i = f_index[op[:3]]
                bk = f_bank[i % 2]
                if op[0] != "W2" or op[3] == 0:
                    free_f(b, i)
                if op[0] == "T2":
                    wait(pe, xn2_done, b, G * GT, (g + 1) * GT)
                    for k in range(KD):
                        for t in range(GT):
                            last = te.transpose(bk[:, k * GN + t * P:k * GN + (t + 1) * P],
                                                xn2[:, t, k * P:(k + 1) * P], ident[:, :])
                    last.then_inc(f_ready, 1)
                if op[0] == "LG":
                    wait(pe, f_dve, b, NFD, f_dve_no[("T2", g)])
                    three_pass(bk[0:E, 0:GN], lambda k: wr_hi[:, k, :], lambda k: wr_lo[:, k, :],
                               lambda k: x2_hi[:, k, :], lambda k: x2_lo[:, k, :]).then_inc(f_ready, 1)
                if op[0] == "LT":
                    wait(pe, f_act, b, NFA, f_act_no[("LG", g)], apart=True)
                    for t in range(GT):
                        last = te.transpose(bk[:, t * E:(t + 1) * E], lgt[:, t * P:(t + 1) * P], ident[0:E, 0:E])
                    last.then_inc(f_ready, 1)
                if op[0] == "CT":
                    wait(pe, cw_c, b, G * 5, (g + 1) * 5)
                    for t in range(GT):
                        last = te.transpose(bk[0:C3, t * P:(t + 1) * P], cst[:, t, :].bitcast(F32), ident[:, :])
                    last.then_inc(f_ready, 1)
                if op[0] == "CB":
                    if op[2] == 0:
                        wait(pe, f_dve, b, NFD, f_dve_no[("CT", g)])
                    for j, e in enumerate(range(2 * op[2], min(2 * op[2] + 2, E1))):
                        last = te.matmul(bk[:, j * GN:(j + 1) * GN], spread(sel[:, e:e + 1], P), ct[:, :],
                                         start=True, stop=True)
                    last.then_inc(f_ready, 1)
                if op[0] == "W1":
                    cols = slice(op[2] * H, (op[2] + 1) * H)
                    three_pass(bk[:, 0:GN], lambda k: w1_hi[:, k, cols], lambda k: w1_lo[:, k, cols],
                               lambda k: x2_hi[:, k, :], lambda k: x2_lo[:, k, :]).then_inc(f_ready, 1)
                if op[0] == "W2":
                    t, part = op[2:]
                    if part == 0:
                        wait(pe, f_dve, b, NFD, f_dve_no[("W1", g, E1 - 1)])
                    for e in range(part * E1 // W2_PARTS, (part + 1) * E1 // W2_PARTS):
                        te.matmul(bk[:, 0:D], hs[:, e, t * P:(t + 1) * P], w2_sb[:, e, :],
                                  start=(e == 0), stop=False)
                    if part == W2_PARTS - 1:
                        te.matmul(bk[:, 0:D], ct[:, t * P:(t + 1) * P], b2_st[:, :], start=False, stop=True)\
                            .then_inc(f_ready, 1)

            streams(pe.Fori, lambda ba, bf: walk(steps, attn_op, expert_op, ba, bf))


prep_pe_no, prep_dve_c = {}, []
for _l in (1, 2):
    prep_pe_no[("t", _l)] = len(prep_pe_no) + 1
    prep_pe_no[("b", _l)] = len(prep_pe_no) + 1
    for _m in range(2):
        for _c in (0, 512):
            prep_pe_no[("C", _l, _m, _c)] = len(prep_pe_no) + 1
            prep_dve_c.append(6 + 2 * _l + len(prep_dve_c) + 1)
prep_pe_no[("r",)] = len(prep_pe_no) + 1
N_DVE_PREP = 6 + 12 + 2 + 1 + 3


def kernel(**inputs):
    import numpy as np
    import concourse.bacc as bacc
    from concourse.bass_utils import run_bass_kernel_spmd as run

    nc = bacc.Bacc("TRN2", target_bir_lowering=False, num_devices=1, dynamic_dma_scratch_size=1024)
    arrays = {}

    def dram(name, a):
        a = np.ascontiguousarray(a)
        arrays[name] = a
        return nc.dram_tensor(name, a.shape, mybir.dt.from_np(a.dtype), kind="ExternalInput").ap()

    a = {k: np.asarray(v) for k, v in inputs.items()}
    x = a["L0_attn_x"]
    args = [
        dram("x", x),
        [dram(f"winT{l}", a[f"L0_attn_Win{l}"].T) for l in range(3)],
        dram("wout0", a["L0_attn_Wout0"]),
        dram("wout1", a["L0_attn_Wout1"]),
        [dram(f"woutT{l}", a[f"L0_attn_Wout{l}"].T) for l in range(3)],
        [dram(f"bin{l}", a[f"L0_attn_bin{l}"].reshape(-1, P).T) for l in range(3)],
        [dram(f"bout{l}", a[f"L0_attn_bout{l}"].reshape(-1, P).T) for l in range(2)]
        + [dram("bout2", a["L0_attn_bout2"])],
        dram("wrT", a["L0_ffn_routing_W"].T),
        dram("ebias", a["L0_ffn_expert_bias"]),
        dram("sw1", a["L0_ffn_sW1"]), dram("sb1", a["L0_ffn_sb1"]),
        dram("sw2", a["L0_ffn_sW2"]), dram("sb2", a["L0_ffn_sb2"]),
        dram("rw1", a["L0_ffn_rW1"]), dram("rb1T", a["L0_ffn_rb1"].T),
        dram("rw2", a["L0_ffn_rW2"]), dram("rb2", a["L0_ffn_rb2"]),
        nc.dram_tensor("out", x.shape, F32, kind="ExternalOutput").ap(),
    ]
    block_kernel(nc, *args)
    r = run(nc, [arrays], core_ids=[0])
    return r.results[0]["out"]
```
